# Optimizing a Trainium2 kernel written in Bass

```python
import numpy as np
import jax
import jax.numpy as jnp

def _softmax(x, axis=-1):
    return jax.nn.softmax(x, axis=axis)

def _gelu(x):
    return jax.nn.gelu(x, approximate=True)

def _silu(x):
    return jax.nn.silu(x)

def _sigmoid(x):
    return jax.nn.sigmoid(x)

def _layernorm(x, axis=-1, eps=1e-05):
    m = jnp.mean(x, axis=axis, keepdims=True)
    v = jnp.var(x, axis=axis, keepdims=True)
    return (x - m) / jnp.sqrt(v + eps)

def _scatter_add(tgt, idx, src, axis=0):
    return tgt.at[idx].add(src)

def _segment_sum(src, seg, n):
    return jax.ops.segment_sum(src, seg, n)
kernel_name = 'mk_prb_d1_jaxref_r8_3fcf5b'

def setup_inputs(seed: int=0):
    np.random.seed(seed)
    _w = jnp.asarray

    def _L0_attn_setup():
        import math
        import jax, jax.numpy as jnp
        import numpy as np
        NUM_HEADS = 32
        NUM_KV_HEADS = 8
        HEAD_DIM = 128
        HIDDEN = 512
        ROPE_THETA = 500000.0
        ROPE_FACTOR = 8.0
        HIGH_FF = 4.0
        LOW_FF = 1.0
        ORIG_MAX_POS = 1024

        def _llama3_inv_freq():
            inv = 1.0 / ROPE_THETA ** (np.arange(0, HEAD_DIM, 2, dtype=np.float32) / HEAD_DIM)
            wavelen = 2.0 * np.pi / inv
            low_wl = ORIG_MAX_POS / LOW_FF
            high_wl = ORIG_MAX_POS / HIGH_FF
            inv_scaled = np.where(wavelen > low_wl, inv / ROPE_FACTOR, inv)
            smooth = (ORIG_MAX_POS / wavelen - LOW_FF) / (HIGH_FF - LOW_FF)
            smoothed = (1.0 - smooth) / ROPE_FACTOR * inv + smooth * inv
            is_medium = (wavelen <= low_wl) & (wavelen >= high_wl)
            return jnp.asarray(np.where(is_medium, smoothed, inv_scaled), dtype=jnp.float32)

        def _rotate_half(x):
            h = x.shape[-1] // 2
            return jnp.concatenate([-x[..., h:], x[..., :h]], axis=-1)
        key = jax.random.key(seed)
        ks = jax.random.split(key, 5)
        s = 0.02
        return {'x': jax.random.normal(ks[0], (1, 256, HIDDEN), dtype=jnp.float32), 'Wq': jax.random.normal(ks[1], (NUM_HEADS * HEAD_DIM, HIDDEN), dtype=jnp.float32) * s, 'Wk': jax.random.normal(ks[2], (NUM_KV_HEADS * HEAD_DIM, HIDDEN), dtype=jnp.float32) * s, 'Wv': jax.random.normal(ks[3], (NUM_KV_HEADS * HEAD_DIM, HIDDEN), dtype=jnp.float32) * s, 'Wo': jax.random.normal(ks[4], (HIDDEN, NUM_HEADS * HEAD_DIM), dtype=jnp.float32) * s}
    _L0_attn_in = _L0_attn_setup()

    def _L0_ffn_setup():
        import jax, jax.numpy as jnp
        import numpy as np
        DIM = 512
        INTER = 128
        E = 16
        GROUPS = 4
        LIM = 2
        K = 2
        SHARED_INTER = 2 * INTER
        SCALE = 1.0
        key = jax.random.key(seed)
        ks = jax.random.split(key, 16)

        def n(k, shape, s=0.02):
            return jax.random.normal(k, shape, jnp.float32) * s
        return {'x': jax.random.normal(ks[0], (1, 256, DIM), jnp.float32), 'router_w': n(ks[1], (DIM, E)), 'router_b': n(ks[2], (E,)), 'router_bias': n(ks[3], (E,), 1.0), 'ew1': n(ks[4], (E, DIM, INTER)), 'eb1': n(ks[5], (E, INTER)), 'ew2': n(ks[6], (E, DIM, INTER)), 'eb2': n(ks[7], (E, INTER)), 'ew3': n(ks[8], (E, INTER, DIM)), 'eb3': n(ks[9], (E, DIM)), 'sw1': n(ks[10], (DIM, SHARED_INTER)), 'sb1': n(ks[11], (SHARED_INTER,)), 'sw2': n(ks[12], (DIM, SHARED_INTER)), 'sb2': n(ks[13], (SHARED_INTER,)), 'sw3': n(ks[14], (SHARED_INTER, DIM)), 'sb3': n(ks[15], (DIM,))}
    _L0_ffn_in = _L0_ffn_setup()
    _d = {'L0_attn_x': _L0_attn_in['x'], 'L0_attn_Wq': _L0_attn_in['Wq'], 'L0_attn_Wk': _L0_attn_in['Wk'], 'L0_attn_Wv': _L0_attn_in['Wv'], 'L0_attn_Wo': _L0_attn_in['Wo'], 'L0_ffn_router_w': _L0_ffn_in['router_w'], 'L0_ffn_router_b': _L0_ffn_in['router_b'], 'L0_ffn_router_bias': _L0_ffn_in['router_bias'], 'L0_ffn_ew1': _L0_ffn_in['ew1'], 'L0_ffn_eb1': _L0_ffn_in['eb1'], 'L0_ffn_ew2': _L0_ffn_in['ew2'], 'L0_ffn_eb2': _L0_ffn_in['eb2'], 'L0_ffn_ew3': _L0_ffn_in['ew3'], 'L0_ffn_eb3': _L0_ffn_in['eb3'], 'L0_ffn_sw1': _L0_ffn_in['sw1'], 'L0_ffn_sb1': _L0_ffn_in['sb1'], 'L0_ffn_sw2': _L0_ffn_in['sw2'], 'L0_ffn_sb2': _L0_ffn_in['sb2'], 'L0_ffn_sw3': _L0_ffn_in['sw3'], 'L0_ffn_sb3': _L0_ffn_in['sb3']}
    _x0 = _d['L0_attn_x']
    _d['L0_attn_x'] = jax.random.normal(jax.random.fold_in(jax.random.key(seed), 1), (2, 512, 512), dtype=_x0.dtype)
    del _x0
    return _d

def reference(L0_attn_x, L0_attn_Wq, L0_attn_Wk, L0_attn_Wv, L0_attn_Wo, L0_ffn_router_w, L0_ffn_router_b, L0_ffn_router_bias, L0_ffn_ew1, L0_ffn_eb1, L0_ffn_ew2, L0_ffn_eb2, L0_ffn_ew3, L0_ffn_eb3, L0_ffn_sw1, L0_ffn_sb1, L0_ffn_sw2, L0_ffn_sb2, L0_ffn_sw3, L0_ffn_sb3):

    def _L0_attn_ref(x, Wq, Wk, Wv, Wo):
        import math
        import jax, jax.numpy as jnp
        import numpy as np
        NUM_HEADS = 32
        NUM_KV_HEADS = 8
        HEAD_DIM = 128
        HIDDEN = 512
        ROPE_THETA = 500000.0
        ROPE_FACTOR = 8.0
        HIGH_FF = 4.0
        LOW_FF = 1.0
        ORIG_MAX_POS = 1024

        def _llama3_inv_freq():
            inv = 1.0 / ROPE_THETA ** (np.arange(0, HEAD_DIM, 2, dtype=np.float32) / HEAD_DIM)
            wavelen = 2.0 * np.pi / inv
            low_wl = ORIG_MAX_POS / LOW_FF
            high_wl = ORIG_MAX_POS / HIGH_FF
            inv_scaled = np.where(wavelen > low_wl, inv / ROPE_FACTOR, inv)
            smooth = (ORIG_MAX_POS / wavelen - LOW_FF) / (HIGH_FF - LOW_FF)
            smoothed = (1.0 - smooth) / ROPE_FACTOR * inv + smooth * inv
            is_medium = (wavelen <= low_wl) & (wavelen >= high_wl)
            return jnp.asarray(np.where(is_medium, smoothed, inv_scaled), dtype=jnp.float32)

        def _rotate_half(x):
            h = x.shape[-1] // 2
            return jnp.concatenate([-x[..., h:], x[..., :h]], axis=-1)
        B, T, _ = x.shape
        G = NUM_HEADS // NUM_KV_HEADS
        q = jnp.einsum('bth,oh->bto', x, Wq).reshape(B, T, NUM_HEADS, HEAD_DIM).transpose(0, 2, 1, 3)
        k = jnp.einsum('bth,oh->bto', x, Wk).reshape(B, T, NUM_KV_HEADS, HEAD_DIM).transpose(0, 2, 1, 3)
        v = jnp.einsum('bth,oh->bto', x, Wv).reshape(B, T, NUM_KV_HEADS, HEAD_DIM).transpose(0, 2, 1, 3)
        inv_freq = _llama3_inv_freq()
        pos = jnp.arange(T, dtype=jnp.float32)
        freqs = pos[:, None] * inv_freq[None, :]
        emb = jnp.concatenate([freqs, freqs], axis=-1)
        cos, sin = (jnp.cos(emb), jnp.sin(emb))
        q = q * cos + _rotate_half(q) * sin
        k = k * cos + _rotate_half(k) * sin
        qg = q.reshape(B, NUM_KV_HEADS, G, T, HEAD_DIM)
        scale = 1.0 / math.sqrt(HEAD_DIM)
        scores = jnp.einsum('bkgtd,bksd->bkgts', qg, k) * scale
        causal = jnp.tril(jnp.ones((T, T), dtype=bool))
        scores = jnp.where(causal, scores, -jnp.inf)
        attn = jax.nn.softmax(scores, axis=-1)
        out = jnp.einsum('bkgts,bksd->bkgtd', attn, v)
        out = out.reshape(B, NUM_HEADS, T, HEAD_DIM).transpose(0, 2, 1, 3).reshape(B, T, NUM_HEADS * HEAD_DIM)
        return jnp.einsum('bto,ho->bth', out, Wo)

    def _L0_ffn_ref(x, router_w, router_b, router_bias, ew1, eb1, ew2, eb2, ew3, eb3, sw1, sb1, sw2, sb2, sw3, sb3):
        import jax, jax.numpy as jnp
        import numpy as np
        DIM = 512
        INTER = 128
        E = 16
        GROUPS = 4
        LIM = 2
        K = 2
        SHARED_INTER = 2 * INTER
        SCALE = 1.0
        shape = x.shape
        xt = x.reshape(-1, DIM)
        T = xt.shape[0]
        logits = xt @ router_w + router_b
        scores = jax.nn.softmax(logits.astype(jnp.float32), axis=-1) + router_bias
        g = scores.reshape(T, GROUPS, E // GROUPS)
        _, gidx = jax.lax.top_k(g.max(axis=-1), LIM)
        keep = jnp.zeros((T, GROUPS), bool).at[jnp.arange(T)[:, None], gidx].set(True)
        masked = jnp.where(keep[:, :, None], g, -jnp.inf).reshape(T, E)
        _, idx = jax.lax.top_k(masked, K)
        vals = (jnp.take_along_axis(scores, idx, axis=1) * SCALE).astype(x.dtype)
        gate = jnp.zeros((T, E), x.dtype).at[jnp.arange(T)[:, None], idx].add(vals)

        def step(y, p):
            w1, b1, w2, b2, w3, b3, ge = p
            h = jax.nn.silu(xt @ w1 + b1) * (xt @ w2 + b2)
            return (y + ge[:, None] * (h @ w3 + b3), None)
        y, _ = jax.lax.scan(step, jnp.zeros_like(xt), (ew1, eb1, ew2, eb2, ew3, eb3, gate.T))
        z = jax.nn.silu(xt @ sw1 + sb1) * (xt @ sw2 + sb2) @ sw3 + sb3
        return (y + z).reshape(shape)
    x = L0_attn_x
    xn = _layernorm(x, axis=-1)
    x = x + _L0_attn_ref(xn, L0_attn_Wq, L0_attn_Wk, L0_attn_Wv, L0_attn_Wo) + _L0_ffn_ref(xn, L0_ffn_router_w, L0_ffn_router_b, L0_ffn_router_bias, L0_ffn_ew1, L0_ffn_eb1, L0_ffn_ew2, L0_ffn_eb2, L0_ffn_ew3, L0_ffn_eb3, L0_ffn_sw1, L0_ffn_sb1, L0_ffn_sw2, L0_ffn_sb2, L0_ffn_sw3, L0_ffn_sb3)
    return x

_drawn_inputs = setup_inputs


def setup_inputs(seed=0):
    import zlib

    import numpy as np

    out = dict(_drawn_inputs(seed))
    spreads = {}
    factors = {'L0_attn_Wq': 4.271,
     'L0_attn_Wk': 4.181,
     'L0_ffn_router_w': 8.0,
     'L0_ffn_router_b': 184.084,
     'L0_ffn_eb1': 8.0,
     'L0_ffn_eb2': 8.0,
     'L0_ffn_sb1': 36.075,
     'L0_ffn_sb2': 34.934,
     'L0_ffn_sb3': 2.862}
    for name, (base, spread) in spreads.items():
        noise = np.random.default_rng([zlib.crc32(name.encode()), seed]).standard_normal(out[name].shape)
        drawn = base * np.exp(spread * noise) if base else spread * noise
        out[name] = jnp.asarray(drawn.astype(out[name].dtype))
    for name, factor in factors.items():
        out[name] = (out[name] * factor).astype(out[name].dtype)
    return out
```

```python
from contextlib import ExitStack

import numpy as np

import concourse.bass as bass
from concourse import mybir

F32 = mybir.dt.float32
F32R = mybir.dt.float32r
BF16 = mybir.dt.bfloat16
ALU = mybir.AluOpType
ACT = mybir.ActivationFunctionType
AX_X = mybir.AxisListType.X

P = 128
B, T, D = 2, 512, 512
TB = T // P
NB = B * TB
HC = D // P
HEADS, KV = 32, 8
G = HEADS // KV
E, GROUPS, TOPG, TOPK = 16, 4, 2, 2
EG = E // GROUPS
SLOTS = E + 2
PAIRS = SLOTS // 2
EPS = 1e-5
BIG = 3.0e38
MASKED = -1.0e38

TR_BANKS, ROUTE_BANK, GATE_BANKS = (0, 1), 2, (3, 4)
UP_BANKS, LIN_BANKS, DOWN_BANKS = (0, 1), (2, 3), (4, 5)
S_BANKS, PROJ_BANK, OUT_BANK, PT_BANKS, OT_BANK = (0, 1, 2), 3, 4, (5, 6), 7

SHARE = [((0, 1), (2, 3)), ((0, 1), (2, 3)), ((0,), (1,), (2,), (3,)), ((0,), (1,), (2,), (3,))]
USES = 12
USE0 = [0, 2, 4, 8]
TRS = 10
TR0 = [0, 1, 3, 6]

Q_SLOT, Q_ORDER = (4, 0, 1, 3), (1, 2, 3, 5)
K_SLOT, K_ORDER, V_SLOT, V_ORDER = 2, 4, 4, 6


def wait_count(eng, sem, value):
    if not isinstance(value, int) or value > 0:
        eng.wait_ge(sem, value)


def count(per_step, g, b, k):
    return (2 * per_step) * g + (per_step * b + k)


def build(nc, x, wq, wk, wv, wo, experts, eb3, router_w, router_b, router_bias,
          q_cos, q_sin, k_rot, out):
    gate_rows = nc.dram_tensor("gate_rows", (SLOTS, B * T), F32).ap()
    xt = x.rearrange("(n p) d -> n p d", p=P)
    ot = out.rearrange("(n p) d -> n p d", p=P)

    with ExitStack() as ctx:
        def sb(name, shape, dt=F32, stack=ctx):
            return stack.enter_context(nc.sbuf_tensor(name, shape, dt))

        def sem(name):
            return ctx.enter_context(nc.semaphore(name))

        y = sb("y", [P, NB, D])
        xT_hi = sb("xT_hi", [P, HC, B * T], F32R)
        xT_lo = sb("xT_lo", [P, HC, B * T], F32R)
        ident = sb("ident", [P, P])
        ident16 = sb("ident16", [P, P], BF16)
        causal = sb("causal", [P, P], BF16)
        bank = [ctx.enter_context(nc.psum_tensor(f"bank{i}", [P, 512], F32)) for i in range(8)]

        early = ExitStack()
        xn = sb("xn", [P, NB, D], stack=early)
        stats = sb("stats", [P, NB, 6], stack=early)
        mv = sb("mv", [P, NB, 2], stack=early)
        lnt = sb("lnt", [P, 4, NB], stack=early)
        rw = sb("rw", [P, HC, E], stack=early)
        rw_hi = sb("rw_hi", [P, HC, E], F32R, early)
        rw_lo = sb("rw_lo", [P, HC, E], F32R, early)
        rb = sb("rb", [P, 2, E], stack=early)
        route = sb("route", [P, 3, NB, E], stack=early)
        score, masked, chosen = route[:, 0], route[:, 1], route[:, 2]
        red = sb("red", [P, 3, NB], stack=early)
        grp = sb("grp", [P, 3, NB, GROUPS], stack=early)
        beat = sb("beat", [P, 2, NB, E, E], stack=early)
        before = sb("before", [P, E, E], stack=early)
        gates = sb("gates", [P, NB, P], stack=early)
        gT = sb("gT", [P, B * T], stack=early)
        gT_hi = sb("gT_hi", [P, B * T], F32R, early)
        gT_lo = sb("gT_lo", [P, B * T], F32R, early)
        b3 = sb("b3", [P, D], stack=early)
        b3_hi = sb("b3_hi", [P, D], F32R, early)
        b3_lo = sb("b3_lo", [P, D], F32R, early)
        eraw = sb("eraw", [P, 2, 3 * D + 2], stack=early)
        ew_hi = sb("ew_hi", [P, 2, 3, D], F32R, early)
        ew_lo = sb("ew_lo", [P, 2, 3, D], F32R, early)
        ebias = sb("ebias", [P, 2, 2], stack=early)
        gate = sb("gate", [P, 2, B * T], stack=early)
        act_out = sb("act_out", [P, 2, T], stack=early)
        hid = sb("hid", [P, 2, T], stack=early)
        h_hi = sb("h_hi", [P, 2, B, T], F32R, early)
        h_lo = sb("h_lo", [P, 2, B, T], F32R, early)
        early.close()

        qc = sb("qc", [P, T])
        qs = sb("qs", [P, T])
        kr = sb("kr", [P, TB, 3, 64])
        raw = sb("raw", [P, 5, D])
        wq_hi = sb("wq_hi", [P, G, D], F32R)
        wq_lo = sb("wq_lo", [P, G, D], F32R)
        wkv_hi = sb("wkv_hi", [P, HC, 2, P], F32R)
        wkv_lo = sb("wkv_lo", [P, HC, 2, P], F32R)
        wo_hi = sb("wo_hi", [P, G, D], F32R)
        wo_lo = sb("wo_lo", [P, G, D], F32R)
        q_hi = sb("q_hi", [P, B, G, T], F32R)
        q_lo = sb("q_lo", [P, B, G, T], F32R)
        kT_hi = sb("kT_hi", [P, B, T], F32R)
        kT_lo = sb("kT_lo", [P, B, T], F32R)
        v_hi = sb("v_hi", [P, B, TB, P], F32R)
        v_lo = sb("v_lo", [P, B, TB, P], F32R)
        rot = sb("rot", [P, 3, T])
        krot = sb("krot", [P, 2, 2, P])
        ksum = sb("ksum", [P, TB, P])
        prob = sb("prob", [P, G, T])
        pT_hi = sb("pT_hi", [P, 2, G * P], F32R)
        pT_lo = sb("pT_lo", [P, 2, G * P], F32R)
        oT_hi = sb("oT_hi", [P, 2, G, P], F32R)
        oT_lo = sb("oT_lo", [P, 2, G, P], F32R)
        nmax = sb("nmax", [P, TB * G])
        psum_row = sb("psum_row", [P, TB * G])
        rsum = sb("rsum", [P, TB * G])

        x_in = [sem(f"x_in{i}") for i in range(NB)]
        small_in = sem("small_in")
        b3_zero = sem("b3_zero")
        consts = sem("consts")
        chain = sem("chain")
        var_ready, std_ready = sem("var_ready"), sem("std_ready")
        xn_ready, xT_psum, xT_hi_ok, xT_ok = sem("xn_ready"), sem("xT_psum"), sem("xT_hi_ok"), sem("xT_ok")
        rw_ok, logits_ok, shifted_ok, exp_ok = sem("rw_ok"), sem("logits_ok"), sem("shifted_ok"), sem("exp_ok")
        gates_ok, gT_psum, gT_copied, gT_ok = sem("gates_ok"), sem("gT_psum"), sem("gT_copied"), sem("gT_ok")
        gate_stored, b3_psum, b3_added = sem("gate_stored"), sem("b3_psum"), sem("b3_added")
        eraw_in = [sem(f"eraw_in{s}") for s in range(2)]
        gate_in = [sem(f"gate_in{s}") for s in range(2)]
        ew_hi_ok, ew_split = sem("ew_hi_ok"), sem("ew_split")
        up_psum, silu_ok, lin_ok, h_ok = sem("up_psum"), sem("silu_ok"), sem("lin_ok"), sem("h_ok")
        h_hi_ok, h_split, down_psum, down_added = sem("h_hi_ok"), sem("h_split"), sem("down_psum"), sem("down_added")
        tables_in = sem("tables_in")
        raw_in = [sem(f"raw_in{s}") for s in range(5)]
        w_hi_ok, w_split, wo_hi_ok, wo_split = sem("w_hi_ok"), sem("w_split"), sem("wo_hi_ok"), sem("wo_split")
        q_psum, q_turned, q_summed, q_hi_ok, q_split = (sem(n) for n in ("q_psum", "q_turned", "q_summed", "q_hi_ok", "q_split"))
        kv_psum, k_turned, k_summed, v_hi_ok, v_split = (sem(n) for n in ("kv_psum", "k_turned", "k_summed", "v_hi_ok", "v_split"))
        kT_psum, kT_hi_ok, kT_split = sem("kT_psum"), sem("kT_hi_ok"), sem("kT_split")
        s_psum, max_ok, exps_ok, rsum_ok, prob_ok = (sem(n) for n in ("s_psum", "max_ok", "exps_ok", "rsum_ok", "prob_ok"))
        pT_psum, pT_hi_ok, pT_split, pv_done = (sem(n) for n in ("pT_psum", "pT_hi_ok", "pT_split", "pv_done"))
        oT_hi_ok, oT_split, o_psum, o_added = (sem(n) for n in ("oT_hi_ok", "oT_split", "o_psum", "o_added"))
        stored = sem("stored")
        pool_free = sem("pool_free")

        block = ctx.enter_context(nc.Block())
        EXPERTS_DONE = 8 * PAIRS

        @block.sync
        def _(sp):
            for n in range(NB):
                sp.dma_start(y[:, n, :], xt[n]).then_inc(x_in[n], 16)
            sp.dma_start(rw[:, :, :], router_w.rearrange("(c p) e -> p c e", p=P)).then_inc(small_in, 16)
            sp.dma_start(rb[:, 0, :], router_b.partition_broadcast(P)).then_inc(small_in, 16)
            sp.dma_start(rb[:, 1, :], router_bias.partition_broadcast(P)).then_inc(small_in, 16)
            sp.wait_ge(b3_zero, 1)
            sp.dma_start(b3[0:E + 1, :], eb3).then_inc(small_in, 16)

            for s in range(2):
                sp.dma_start(eraw[:, s, :], experts[s]).then_inc(eraw_in[s], 16)
            sp.wait_ge(gT_copied, 1)
            sp.dma_start(gate_rows, gT[0:SLOTS, :]).then_inc(gate_stored, 16)
            sp.wait_ge(gate_stored, 16)
            for s in range(2):
                sp.dma_start(gate[:, s, :], gate_rows[s, :].partition_broadcast(P)).then_inc(gate_in[s], 16)
            with sp.Fori(1, PAIRS) as q:
                for s in range(2):
                    sp.wait_ge(ew_split, 6 * q + (s - 1))
                    sp.dma_start(eraw[:, s, :], experts[bass.ds(2 * q + s, 1), :, :].rearrange("a p n -> (a p) n"))\
                      .then_inc(eraw_in[s], 16)
                for s in range(2):
                    sp.wait_ge(lin_ok, 4 * q + (s - 1))
                    sp.dma_start(gate[:, s, :], gate_rows[bass.ds(2 * q + s, 1), :].partition_broadcast(P)
                                 .rearrange("p a t -> p (a t)")).then_inc(gate_in[s], 16)

            sp.wait_ge(down_added, EXPERTS_DONE)
            sp.dma_start(qc[:, :], q_cos).then_inc(tables_in, 16)
            sp.dma_start(qs[:, :], q_sin).then_inc(tables_in, 16)
            sp.dma_start(kr[:, :, :, :], k_rot).then_inc(tables_in, 16)

            def load(slot, src):
                sp.dma_start(raw[:, slot, :], src).then_inc(raw_in[slot], 16)

            for h in range(3):
                load(Q_SLOT[h], wq[h])
            load(K_SLOT, wk[0])
            load(Q_SLOT[3], wq[3])
            sp.wait_ge(w_split, 1)
            load(V_SLOT, wv[0])

            def key_head(g, more):
                def row(t, n):
                    return t[bass.ds(n, 1), :, :].rearrange("a p n -> (a p) n")
                for c, order in enumerate((2, 3, 4, 5)):
                    sp.wait_ge(w_split, 6 * g + order)
                    load(c, row(wo, G * g + c))
                if more:
                    sp.wait_ge(w_split, 6 * g + V_ORDER)
                    load(Q_SLOT[0], row(wq, G * g + G))
                    for h in (1, 2):
                        sp.wait_ge(wo_split, 4 * g + h)
                        load(Q_SLOT[h], row(wq, G * g + (G + h)))
                    sp.wait_ge(wo_split, 4 * g + 3)
                    load(K_SLOT, row(wk, g + 1))
                    sp.wait_ge(wo_split, 4 * g + 4)
                    load(Q_SLOT[3], row(wq, G * g + (G + 3)))
                    sp.wait_ge(w_split, 6 * g + 7)
                    load(V_SLOT, row(wv, g + 1))

            with sp.Fori(0, KV - 1) as g:
                key_head(g, True)
            key_head(KV - 1, False)

            for n in range(NB):
                sp.wait_ge(o_added, 8 * (KV - 1) + n + 1)
                sp.dma_start(ot[n], y[:, n, :]).then_inc(stored, 16)
            sp.wait_ge(stored, 16 * NB)

        @block.gpsimd
        def _(pool):
            nc.gpsimd.memset(ident[:, :], 0.0).then_inc(consts, 1)
            nc.gpsimd.memset(ident16[:, :], 0.0).then_inc(consts, 1)
            nc.gpsimd.memset(causal[:, :], 0.0).then_inc(consts, 1)
            nc.gpsimd.memset(before[:, :, :], 1.0).then_inc(consts, 1)
            pool.wait_ge(consts, 4)
            for m in (ident, ident16):
                nc.gpsimd.affine_select(out=m[:, :], in_=m[:, :], compare_op=ALU.not_equal, fill=1.0, base=0,
                                        pattern=[[-1, P]], channel_multiplier=1).then_inc(consts, 1)
            nc.gpsimd.affine_select(out=causal[:, :], in_=causal[:, :], compare_op=ALU.is_ge, fill=MASKED, base=0,
                                    pattern=[[-1, P]], channel_multiplier=1).then_inc(consts, 1)
            nc.gpsimd.affine_select(out=before[:, :, :], in_=before[:, :, :], compare_op=ALU.is_gt, fill=0.0, base=0,
                                    pattern=[[1, E], [-1, E]], channel_multiplier=0).then_inc(consts, 1)

            def split(hi, lo, src, hi_ok, lo_ok, n):
                nc.gpsimd.tensor_scalar(hi, src, 1.0, 1.0, ALU.mult, ALU.mult).then_inc(hi_ok, 1)
                pool.wait_ge(hi_ok, n)
                nc.gpsimd.tensor_tensor(lo, src, hi.bitcast(F32), ALU.subtract).then_inc(lo_ok, 1)

            def expert_weights(q):
                for s in range(2):
                    pool.wait_ge(eraw_in[s], 16 * q + 16)
                    wait_count(pool, up_psum, 4 * q + (s - 1))
                    wait_count(pool, silu_ok, 4 * q + (s - 1))
                    wait_count(pool, lin_ok, 4 * q + (s - 1))
                    pool.sem_inc(pool_free, 1)
                    nc.gpsimd.tensor_copy(ebias[:, s, :], eraw[:, s, 3 * D:3 * D + 2])
                    for m in range(2):
                        split(ew_hi[:, s, m, :], ew_lo[:, s, m, :], eraw[:, s, m * D:(m + 1) * D],
                              ew_hi_ok, ew_split, 6 * q + (2 * s + m + 1))
                for s in range(2):
                    wait_count(pool, down_psum, 8 * q)
                    pool.sem_inc(pool_free, 1)
                    split(ew_hi[:, s, 2, :], ew_lo[:, s, 2, :], eraw[:, s, 2 * D:3 * D],
                          ew_hi_ok, ew_split, 6 * q + (5 + s))

            expert_weights(0)
            with pool.Fori(1, PAIRS) as q:
                expert_weights(q)

            def add_q(g, b, h):
                pool.wait_ge(q_turned, count(4, g, b, h + 1))
                wait_count(pool, q_split, count(4, g, b, h))
                nc.gpsimd.tensor_tensor(rot[:, 2, :], rot[:, 0, :], rot[:, 1, :], ALU.add).then_inc(q_summed, 1)

            def add_k(g, b, i):
                pool.wait_ge(k_turned, count(2, g, b, i + 1))
                nc.gpsimd.tensor_tensor(ksum[:, 2 * i:2 * i + 2, :], krot[:, 0], krot[:, 1], ALU.add)\
                    .then_inc(k_summed, 1)

            def split_q(g, h, used):
                wait_count(pool, q_psum, used)
                pool.wait_ge(raw_in[Q_SLOT[h]], 32 * g + 16)
                pool.sem_inc(pool_free, 1)
                split(wq_hi[:, h, :], wq_lo[:, h, :], raw[:, Q_SLOT[h], :], w_hi_ok, w_split, 6 * g + Q_ORDER[h])

            def split_kv(g, kv, used):
                slot, order = ((K_SLOT, K_ORDER), (V_SLOT, V_ORDER))[kv]
                wait_count(pool, kv_psum, used)
                pool.wait_ge(raw_in[slot], 32 * g + (16, 32)[kv])
                pool.sem_inc(pool_free, 1)
                src = raw[:, slot, :].rearrange("p (c o) -> p c o", c=HC)
                split(wkv_hi[:, :, kv, :], wkv_lo[:, :, kv, :], src, w_hi_ok, w_split, 6 * g + order)

            def normalise(g, b, i):
                pool.wait_ge(rsum_ok, count(4, g, b, i + 1))
                pool.sem_inc(pool_free, 1)
                for h in range(G):
                    row = prob[:, h, 0:P * (i + 1)]
                    last = nc.gpsimd.tensor_scalar(row, row, rsum[:, G * i + h:G * i + h + 1], 1.0, ALU.mult, ALU.mult)
                last.then_inc(prob_ok, 1)

            pool.wait_ge(down_added, EXPERTS_DONE)
            split_q(0, 0, 0)
            split_q(0, 1, 0)
            split_q(0, 2, 0)
            split_kv(0, 0, 0)
            split_q(0, 3, 0)
            split_kv(0, 1, 0)
            for i in range(TB):
                add_q(0, 0, i)
                if i < 2:
                    add_k(0, 0, i)

            def step(g, b, more):
                ng, nb = (g, 1) if b == 0 else (g + 1, 0)
                for i in range(TB):
                    normalise(g, b, i)
                    if more or b == 0:
                        add_q(ng, nb, i)
                        if i < 2:
                            add_k(ng, nb, i)
                    if b == 0 and more:
                        split_q(g + 1, i, count(4, g, 1, i + 1)) if i < 3 else None
                        if i == 2:
                            split_kv(g + 1, 0, count(2, g, 1, 2))
                        if i == 3:
                            split_q(g + 1, 3, count(4, g, 1, 4))
                            split_kv(g + 1, 1, count(2, g, 1, 2))

            with pool.Fori(0, KV - 1) as g:
                step(g, 0, True)
                step(g, 1, True)
            step(KV - 1, 0, False)
            step(KV - 1, 1, False)

        @block.scalar
        def _(act):
            act.wait_ge(var_ready, 1)
            nc.scalar.activation(lnt[:, 1, :], lnt[:, 0, :], ACT.Sqrt).then_inc(std_ready, 1)
            for n in range(B * HC):
                c, b = n % HC, n // HC
                act.wait_ge(xT_psum, n + 1)
                nc.scalar.activation(xT_hi[:, c, b * T:(b + 1) * T], bank[TR_BANKS[n % 2]][:, :], ACT.Copy)\
                    .then_inc(xT_hi_ok, 1)
            act.wait_ge(shifted_ok, 1)
            nc.scalar.activation(score, score, ACT.Exp).then_inc(exp_ok, 1)
            act.wait_ge(gT_psum, 1)
            for j in range(2):
                last = nc.scalar.activation(gT[:, j * T:(j + 1) * T], bank[GATE_BANKS[j]][:, :], ACT.Copy)
            last.then_inc(gT_copied, 1)

            def pair(q):
                for t in range(4):
                    s, b = t % 2, t // 2
                    act.wait_ge(up_psum, 4 * q + (t + 1))
                    wait_count(act, h_ok, 4 * q + (t - 1))
                    nc.scalar.activation(act_out[:, t % 2, :], bank[UP_BANKS[t % 2]][:, :], ACT.Silu,
                                         bias=ebias[:, s, 0:1]).then_inc(silu_ok, 1)
                    act.wait_ge(h_ok, 4 * q + (t + 1))
                    nc.scalar.activation(h_hi[:, s, b, :], hid[:, t % 2, :], ACT.Copy).then_inc(h_hi_ok, 1)

            pair(0)
            with act.Fori(1, PAIRS) as q:
                pair(q)

            act.wait_ge(down_added, EXPERTS_DONE)

            def hi_q(g, b, h):
                act.wait_ge(q_summed, count(4, g, b, h + 1))
                nc.scalar.activation(q_hi[:, b, h, :], rot[:, 2, :], ACT.Copy).then_inc(q_hi_ok, 1)

            def hi_v(g, b, i):
                act.wait_ge(k_turned, count(2, g, b, i + 1))
                src = bank[PROJ_BANK].rearrange("p (n k o) -> p n k o", n=2, k=2)[:, :, 1, :]
                nc.scalar.activation(v_hi[:, b, 2 * i:2 * i + 2, :], src, ACT.Copy).then_inc(v_hi_ok, 1)

            def hi_kT(g, b):
                act.wait_ge(kT_psum, count(1, g, b, 1))
                nc.scalar.activation(kT_hi[:, b, :], bank[PROJ_BANK][:, :], ACT.Copy).then_inc(kT_hi_ok, 1)

            def exps(g, b, i):
                for m, heads in enumerate(SHARE[i]):
                    use = USE0[i] + m
                    act.wait_ge(max_ok, count(USES, g, b, use + 1))
                    for k, h in enumerate(heads):
                        col = slice(G * i + h, G * i + h + 1)
                        last = nc.scalar.activation(prob[:, h, 0:P * (i + 1)],
                                                    bank[S_BANKS[use % 3]][:, 256 * k:256 * k + P * (i + 1)], ACT.Exp,
                                                    bias=nmax[:, col], accum_out=psum_row[:, col])
                    last.then_inc(exps_ok, 1)

            def hi_oT(pg, pb, pi):
                act.wait_ge(pv_done, count(TRS, pg, pb, TR0[pi] + pi + 1))
                wait_count(act, o_psum, count(4, pg, pb, pi - 1))
                nc.scalar.activation(oT_hi[:, pi % 2], bank[OT_BANK].rearrange("p (h t) -> p h t", h=G), ACT.Copy)\
                    .then_inc(oT_hi_ok, 1)

            def hi_pT(g, b, n):
                act.wait_ge(pT_psum, count(TRS, g, b, n + 1))
                wait_count(act, pv_done, count(TRS, g, b, n - 1))
                nc.scalar.activation(pT_hi[:, n % 2, :], bank[PT_BANKS[n % 2]][:, :], ACT.Copy).then_inc(pT_hi_ok, 1)

            for i in range(TB):
                if i < 2:
                    hi_q(0, 0, i)
                    hi_v(0, 0, i)
                elif i == 2:
                    hi_q(0, 0, i)
                    hi_kT(0, 0)
                else:
                    hi_q(0, 0, i)

            def step(g, b, more, first=False):
                ng, nb = (g, 1) if b == 0 else (g + 1, 0)
                for i in range(TB):
                    exps(g, b, i)
                    if i:
                        hi_oT(g, b, i - 1)
                    elif not first:
                        hi_oT(*((g - 1, 1) if b == 0 else (g, 0)), TB - 1)
                    n = TR0[i]
                    for j in range(min(2, i + 1)):
                        hi_pT(g, b, n + j)
                    if more or b == 0:
                        if i < 2:
                            hi_v(ng, nb, i)
                        if i == 2:
                            hi_kT(ng, nb)
                    for j in range(2, i + 1):
                        hi_pT(g, b, n + j)
                    if more or b == 0:
                        hi_q(ng, nb, i)
                    if b == 0 and i == 0:
                        wait_count(act, o_psum, 8 * g)
                        for c in range(G):
                            act.wait_ge(raw_in[c], 32 * g + 32)
                            nc.scalar.activation(wo_hi[:, c, :], raw[:, c, :], ACT.Copy).then_inc(wo_hi_ok, 1)

            step(0, 0, True, first=True)
            step(0, 1, True)
            with act.Fori(1, KV - 1) as g:
                step(g, 0, True)
                step(g, 1, True)
            step(KV - 1, 0, False)
            step(KV - 1, 1, False)
            hi_oT(KV - 1, 1, TB - 1)

        @block.vector
        def _(dve):
            done = [0]

            def link(ins):
                done[0] += 1
                ins.then_inc(chain, 1)
                dve.wait_ge(chain, done[0])

            nc.vector.memset(b3[:, :], 0.0).then_inc(b3_zero, 1)
            link(nc.vector.memset(gates[:, :, :], 0.0))
            link(nc.vector.memset(gates[:, :, E:SLOTS], 1.0))
            for n in range(NB):
                dve.wait_ge(x_in[n], 16)
                last = nc.vector.bn_stats(stats[:, n, :], y[:, n, :])
            link(last)
            for n in range(NB):
                last = nc.vector.bn_aggr(mv[:, n, :], stats[:, n, :])
            link(last)
            var, std, inv, tmp = (lnt[:, k, :] for k in range(4))
            nc.vector.tensor_scalar(var, mv[:, :, 1], EPS, None, ALU.add).then_inc(var_ready, 1)
            dve.wait_ge(std_ready, 1)
            link(nc.vector.reciprocal(inv, std))
            link(nc.vector.tensor_tensor(tmp, inv, inv, ALU.mult))
            link(nc.vector.tensor_tensor(tmp, tmp, var, ALU.mult))
            link(nc.vector.tensor_scalar(tmp, tmp, -0.5, 1.5, ALU.mult, ALU.add))
            link(nc.vector.tensor_tensor(inv, inv, tmp, ALU.mult))
            for n in range(NB):
                nc.vector.tensor_scalar(xn[:, n, :], y[:, n, :], mv[:, n, 0:1], inv[:, n:n + 1],
                                        ALU.subtract, ALU.mult).then_inc(xn_ready, 1)
            dve.wait_ge(small_in, 64)
            link(nc.vector.tensor_copy(rw_hi[:, :, :], rw[:, :, :]))
            nc.vector.tensor_tensor(rw_lo[:, :, :], rw[:, :, :], rw_hi[:, :, :].bitcast(F32), ALU.subtract)\
                .then_inc(rw_ok, 1)
            link(nc.vector.tensor_copy(b3_hi[:, :], b3[:, :]))
            link(nc.vector.tensor_tensor(b3_lo[:, :], b3[:, :], b3_hi[:, :].bitcast(F32), ALU.subtract))
            for n in range(B * HC):
                c, b = n % HC, n // HC
                span = slice(b * T, (b + 1) * T)
                dve.wait_ge(xT_hi_ok, n + 1)
                nc.vector.tensor_tensor(xT_lo[:, c, span], bank[TR_BANKS[n % 2]][:, :], xT_hi[:, c, span].bitcast(F32),
                                        ALU.subtract).then_inc(xT_ok, 1)

            def over_blocks(row):
                return row.unsqueeze(1).broadcast_to([P, NB, E])

            def over_experts(col):
                return col.unsqueeze(2).broadcast_to([P, NB, E])

            dve.wait_ge(logits_ok, 1)
            logits = bank[ROUTE_BANK][:, 0:NB * E].rearrange("p (n e) -> p n e", n=NB)
            link(nc.vector.tensor_tensor(score, logits, over_blocks(rb[:, 0, :]), ALU.add))
            link(nc.vector.tensor_reduce(red[:, 0, :], score, AX_X, ALU.max))
            nc.vector.tensor_tensor(score, score, over_experts(red[:, 0, :]), ALU.subtract).then_inc(shifted_ok, 1)
            dve.wait_ge(exp_ok, 1)
            link(nc.vector.tensor_reduce(red[:, 1, :], score, AX_X, ALU.add))
            link(nc.vector.reciprocal(red[:, 2, :], red[:, 1, :]))
            link(nc.vector.tensor_tensor(score, score, over_experts(red[:, 2, :]), ALU.mult))
            link(nc.vector.tensor_tensor(score, score, over_blocks(rb[:, 1, :]), ALU.add))

            def top(result, v, n, k):
                v_i = v.unsqueeze(3).broadcast_to([P, NB, n, n])
                v_j = v.unsqueeze(2).broadcast_to([P, NB, n, n])
                more, same = beat[:, 0, :, 0:n, 0:n], beat[:, 1, :, 0:n, 0:n]
                link(nc.vector.tensor_tensor(more, v_j, v_i, ALU.is_gt))
                link(nc.vector.tensor_tensor(same, v_j, v_i, ALU.is_equal))
                link(nc.vector.tensor_tensor(same, same, before[:, 0:n, 0:n].unsqueeze(1).broadcast_to([P, NB, n, n]),
                                             ALU.mult))
                link(nc.vector.tensor_tensor(more, more, same, ALU.add))
                link(nc.vector.tensor_reduce(result, more, AX_X, ALU.add))
                link(nc.vector.tensor_scalar(result, result, float(k), None, ALU.is_lt))

            dve.wait_ge(consts, 8)
            in_groups = score.rearrange("p n (g e) -> p n g e", g=GROUPS)
            link(nc.vector.tensor_reduce(grp[:, 0], in_groups, AX_X, ALU.max))
            top(grp[:, 1], grp[:, 0], GROUPS, TOPG)
            link(nc.vector.tensor_scalar(grp[:, 2], grp[:, 1], -1.0, BIG, ALU.add, ALU.mult))
            masked_groups = masked.rearrange("p n (g e) -> p n g e", g=GROUPS)
            link(nc.vector.tensor_tensor(masked_groups, in_groups,
                                         grp[:, 1].unsqueeze(3).broadcast_to([P, NB, GROUPS, EG]), ALU.mult))
            link(nc.vector.tensor_tensor(masked_groups, masked_groups,
                                         grp[:, 2].unsqueeze(3).broadcast_to([P, NB, GROUPS, EG]), ALU.add))
            top(chosen, masked, E, TOPK)
            nc.vector.tensor_tensor(gates[:, :, 0:E], score, chosen, ALU.mult).then_inc(gates_ok, 1)
            dve.wait_ge(gT_copied, 1)
            link(nc.vector.tensor_copy(gT_hi[:, :], gT[:, :]))
            nc.vector.tensor_tensor(gT_lo[:, :], gT[:, :], gT_hi[:, :].bitcast(F32), ALU.subtract).then_inc(gT_ok, 1)
            for n in range(NB):
                dve.wait_ge(b3_psum, n + 1)
                nc.vector.tensor_tensor(y[:, n, :], y[:, n, :], bank[DOWN_BANKS[n % 2]][:, :], ALU.add)\
                    .then_inc(b3_added, 1)

            def hidden(q, t):
                s, b = t % 2, t // 2
                h = hid[:, t % 2, :]
                dve.wait_ge(up_psum, 4 * q + (t + 1))
                if b == 0:
                    dve.wait_ge(gate_in[s], 16 * q + 16)
                nc.vector.scalar_tensor_tensor(h, bank[LIN_BANKS[t % 2]][:, :], ebias[:, s, 1:2],
                                               gate[:, s, b * T:(b + 1) * T], ALU.add, ALU.mult).then_inc(lin_ok, 1)
                dve.wait_ge(lin_ok, 4 * q + (t + 1))
                dve.wait_ge(silu_ok, 4 * q + (t + 1))
                nc.vector.tensor_tensor(h, h, act_out[:, t % 2, :], ALU.mult).then_inc(h_ok, 1)
                dve.wait_ge(h_hi_ok, 4 * q + (t + 1))
                nc.vector.tensor_tensor(h_lo[:, s, b, :], h, h_hi[:, s, b, :].bitcast(F32), ALU.subtract)\
                    .then_inc(h_split, 1)

            def add_down(q, b):
                for k in range(TB):
                    n = TB * b + k
                    dve.wait_ge(down_psum, 8 * q + (n + 1))
                    nc.vector.tensor_tensor(y[:, n, :], y[:, n, :], bank[DOWN_BANKS[n % 2]][:, :], ALU.add)\
                        .then_inc(down_added, 1)

            def pair(q, first=False):
                hidden(q, 0)
                hidden(q, 1)
                if not first:
                    add_down(q - 1, 1)
                hidden(q, 2)
                hidden(q, 3)
                add_down(q, 0)

            pair(0, first=True)
            with dve.Fori(1, PAIRS) as q:
                pair(q)
            add_down(PAIRS - 1, 1)

            dve.wait_ge(tables_in, 48)

            def turn_q(g, b, h):
                q = bank[PROJ_BANK]
                dve.wait_ge(q_psum, count(4, g, b, h + 1))
                wait_count(dve, q_summed, count(4, g, b, h))
                nc.vector.tensor_tensor(rot[:, 0, :], q[:, :], qc[:, :], ALU.mult)
                nc.vector.tensor_tensor(rot[0:64, 1, :], q[64:128, :], qs[64:128, :], ALU.mult)
                nc.vector.tensor_tensor(rot[64:128, 1, :], q[0:64, :], qs[0:64, :], ALU.mult).then_inc(q_turned, 1)

            def lo_q(g, b, h):
                dve.wait_ge(q_hi_ok, count(4, g, b, h + 1))
                nc.vector.tensor_tensor(q_lo[:, b, h, :], rot[:, 2, :], q_hi[:, b, h, :].bitcast(F32), ALU.subtract)\
                    .then_inc(q_split, 1)

            def turn_k(g, b, i):
                k = bank[PROJ_BANK].rearrange("p (n k f o) -> p n k f o", n=2, k=2, f=2)[:, :, 0]
                table = kr[:, 2 * i:2 * i + 2]
                one, two = (krot[:, m].rearrange("p n (f o) -> p n f o", f=2) for m in range(2))
                dve.wait_ge(kv_psum, count(2, g, b, i + 1))
                wait_count(dve, k_summed, count(2, g, b, i))
                nc.vector.tensor_tensor(one, k, table[:, :, 0:1, :].broadcast_to([P, 2, 2, 64]), ALU.mult)
                nc.vector.tensor_tensor(two[:, :, 0, :], k[:, :, 1, :], table[:, :, 1, :], ALU.mult)
                nc.vector.tensor_tensor(two[:, :, 1, :], k[:, :, 0, :], table[:, :, 2, :], ALU.mult)\
                    .then_inc(k_turned, 1)

            def lo_v(g, b, i):
                src = bank[PROJ_BANK].rearrange("p (n k o) -> p n k o", n=2, k=2)[:, :, 1, :]
                dve.wait_ge(v_hi_ok, count(2, g, b, i + 1))
                nc.vector.tensor_tensor(v_lo[:, b, 2 * i:2 * i + 2, :], src, v_hi[:, b, 2 * i:2 * i + 2, :].bitcast(F32),
                                        ALU.subtract).then_inc(v_split, 1)

            def lo_kT(g, b):
                dve.wait_ge(kT_hi_ok, count(1, g, b, 1))
                nc.vector.tensor_tensor(kT_lo[:, b, :], bank[PROJ_BANK][:, :], kT_hi[:, b, :].bitcast(F32),
                                        ALU.subtract).then_inc(kT_split, 1)

            def maxima(g, b, i):
                for m, heads in enumerate(SHARE[i]):
                    use, k = USE0[i] + m, len(heads)
                    s = bank[S_BANKS[use % 3]][:, :].rearrange("p (k s) -> p k s", k=k)[:, :, 0:P * (i + 1)]
                    dve.wait_ge(s_psum, count(USES, g, b, use + 1))
                    col = G * i + heads[0]
                    nc.vector.tensor_reduce(nmax[:, col:col + k], s, AX_X, ALU.max, negate=True).then_inc(max_ok, 1)

            def inverse_sums(g, b, i):
                dve.wait_ge(exps_ok, count(USES, g, b, USE0[i] + len(SHARE[i])))
                nc.vector.reciprocal(rsum[:, G * i:G * i + G], psum_row[:, G * i:G * i + G]).then_inc(rsum_ok, 1)

            def lo_oT(pg, pb, pi):
                dve.wait_ge(oT_hi_ok, count(4, pg, pb, pi + 1))
                nc.vector.tensor_tensor(oT_lo[:, pi % 2], bank[OT_BANK].rearrange("p (h t) -> p h t", h=G),
                                        oT_hi[:, pi % 2].bitcast(F32), ALU.subtract).then_inc(oT_split, 1)

            def add_out(pg, pb, pi):
                dve.wait_ge(o_psum, count(4, pg, pb, pi + 1))
                n = TB * pb + pi
                nc.vector.tensor_tensor(y[:, n, :], y[:, n, :], bank[OUT_BANK][:, :], ALU.add).then_inc(o_added, 1)

            def lo_pT(g, b, n):
                dve.wait_ge(pT_hi_ok, count(TRS, g, b, n + 1))
                nc.vector.tensor_tensor(pT_lo[:, n % 2, :], bank[PT_BANKS[n % 2]][:, :],
                                        pT_hi[:, n % 2, :].bitcast(F32), ALU.subtract).then_inc(pT_split, 1)

            for i in range(TB):
                turn_q(0, 0, i)
                lo_q(0, 0, i)
                if i < 2:
                    turn_k(0, 0, i)
                    lo_v(0, 0, i)
                if i == 2:
                    lo_kT(0, 0)

            def step(g, b, more, first=False):
                ng, nb = (g, 1) if b == 0 else (g + 1, 0)
                for i in range(TB):
                    before_this = (g, b, i - 1) if i else (g, 0, TB - 1) if b else (g - 1, 1, TB - 1)
                    any_before = bool(i) or not first
                    maxima(g, b, i)
                    inverse_sums(g, b, i)
                    if any_before:
                        lo_oT(*before_this)
                    if more or b == 0:
                        turn_q(ng, nb, i)
                    if any_before:
                        add_out(*before_this)
                    n = TR0[i]
                    for j in range(min(2, i + 1)):
                        lo_pT(g, b, n + j)
                    if more or b == 0:
                        if i < 2:
                            turn_k(ng, nb, i)
                            lo_v(ng, nb, i)
                        if i == 2:
                            lo_kT(ng, nb)
                    for j in range(2, i + 1):
                        lo_pT(g, b, n + j)
                    if more or b == 0:
                        lo_q(ng, nb, i)
                    if b == 0 and i == 0:
                        for c in range(G):
                            dve.wait_ge(wo_hi_ok, 4 * g + (c + 1))
                            nc.vector.tensor_tensor(wo_lo[:, c, :], raw[:, c, :], wo_hi[:, c, :].bitcast(F32),
                                                    ALU.subtract).then_inc(wo_split, 1)

            step(0, 0, True, first=True)
            step(0, 1, True)
            with dve.Fori(1, KV - 1) as g:
                step(g, 0, True)
                step(g, 1, True)
            step(KV - 1, 0, False)
            step(KV - 1, 1, False)
            lo_oT(KV - 1, 1, TB - 1)
            add_out(KV - 1, 1, TB - 1)

        @block.tensor
        def _(pe):
            def product(dst, terms, stop=True):
                for k, (a_hi, a_lo, c_hi, c_lo) in enumerate(terms):
                    nc.tensor.matmul(dst, a_lo, c_hi, start=k == 0, stop=False)
                    nc.tensor.matmul(dst, a_hi, c_lo, start=False, stop=False)
                    last = nc.tensor.matmul(dst, a_hi, c_hi, start=False, stop=stop and k == len(terms) - 1)
                return last

            pe.wait_ge(consts, 8)
            for n in range(B * HC):
                c, b = n % HC, n // HC
                pe.wait_ge(xn_ready, TB * (b + 1))
                wait_count(pe, xT_ok, n - 1)
                for k in range(TB):
                    last = nc.tensor.transpose(bank[TR_BANKS[n % 2]][:, k * P:(k + 1) * P],
                                               xn[:, TB * b + k, c * P:(c + 1) * P], ident[:, :])
                last.then_inc(xT_psum, 1)
            pe.wait_ge(rw_ok, 1)
            pe.wait_ge(xT_ok, B * HC)
            for n in range(NB):
                cols = slice(n * P, (n + 1) * P)
                last = product(bank[ROUTE_BANK][:, n * E:(n + 1) * E],
                               [(xT_hi[:, c, cols], xT_lo[:, c, cols], rw_hi[:, c, :], rw_lo[:, c, :])
                                for c in range(HC)])
            last.then_inc(logits_ok, 1)
            pe.wait_ge(gates_ok, 1)
            for n in range(NB):
                last = nc.tensor.transpose(bank[GATE_BANKS[n // TB]][:, n % TB * P:(n % TB + 1) * P],
                                           gates[:, n, :], ident[:, :])
            last.then_inc(gT_psum, 1)
            pe.wait_ge(gT_ok, 1)
            for n in range(NB):
                cols = slice(n * P, (n + 1) * P)
                wait_count(pe, b3_added, n - 1)
                product(bank[DOWN_BANKS[n % 2]][:, :],
                        [(gT_hi[:, cols], gT_lo[:, cols], b3_hi[:, :], b3_lo[:, :])]).then_inc(b3_psum, 1)

            def up(q, t):
                s, b = t % 2, t // 2
                span = slice(b * T, (b + 1) * T)
                if b == 0:
                    pe.wait_ge(ew_split, 6 * q + (2 + 2 * s))
                wait_count(pe, silu_ok, 4 * q + (t - 1))
                wait_count(pe, lin_ok, 4 * q + (t - 1))
                for m, banks in enumerate((UP_BANKS, LIN_BANKS)):
                    last = product(bank[banks[t % 2]][:, :],
                                   [(ew_hi[:, s, m, c * P:(c + 1) * P], ew_lo[:, s, m, c * P:(c + 1) * P],
                                     xT_hi[:, c, span], xT_lo[:, c, span]) for c in range(HC)])
                last.then_inc(up_psum, 1)

            def down(q, b):
                pe.wait_ge(h_split, 4 * q + (2 * b + 2))
                if b == 0:
                    pe.wait_ge(ew_split, 6 * q + 6)
                for k in range(TB):
                    n = TB * b + k
                    wait_count(pe, down_added, 8 * q + (n - 1))
                    cols = slice(k * P, (k + 1) * P)
                    product(bank[DOWN_BANKS[n % 2]][:, :],
                            [(h_hi[:, s, b, cols], h_lo[:, s, b, cols], ew_hi[:, s, 2, :], ew_lo[:, s, 2, :])
                             for s in range(2)]).then_inc(down_psum, 1)

            def pair(q, first=False):
                up(q, 0)
                up(q, 1)
                if not first:
                    down(q - 1, 1)
                up(q, 2)
                up(q, 3)
                if first:
                    pe.wait_ge(b3_added, NB)
                down(q, 0)

            pe.wait_ge(xT_ok, B * HC)
            pair(0, first=True)
            with pe.Fori(1, PAIRS) as q:
                pair(q)
            down(PAIRS - 1, 1)

            def project_q(g, b, h, weights):
                span = slice(b * T, (b + 1) * T)
                if weights:
                    pe.wait_ge(w_split, 6 * g + Q_ORDER[h])
                if h == 0:
                    wait_count(pe, q_turned, count(4, g, b, 0))
                elif h < 3:
                    pe.wait_ge(v_split, count(2, g, b, h))
                else:
                    pe.wait_ge(kT_split, count(1, g, b, 1))
                product(bank[PROJ_BANK][:, :],
                        [(wq_hi[:, h, c * P:(c + 1) * P], wq_lo[:, h, c * P:(c + 1) * P],
                          xT_hi[:, c, span], xT_lo[:, c, span]) for c in range(HC)]).then_inc(q_psum, 1)

            def project_kv(g, b, i, weights):
                if weights:
                    pe.wait_ge(w_split, 6 * g + 6)
                pe.wait_ge(q_turned, count(4, g, b, i + 1))
                for k in range(2):
                    n = TB * b + 2 * i + k
                    cols = slice(n * P, (n + 1) * P)
                    last = product(bank[PROJ_BANK][:, k * 2 * P:(k + 1) * 2 * P],
                                   [(xT_hi[:, c, cols], xT_lo[:, c, cols],
                                     wkv_hi[:, c].rearrange("p k o -> p (k o)"),
                                     wkv_lo[:, c].rearrange("p k o -> p (k o)")) for c in range(HC)])
                last.then_inc(kv_psum, 1)

            def transpose_k(g, b):
                pe.wait_ge(q_turned, count(4, g, b, 3))
                pe.wait_ge(k_summed, count(2, g, b, 2))
                for k in range(TB):
                    last = nc.tensor.transpose(bank[PROJ_BANK][:, k * P:(k + 1) * P], ksum[:, k, :], ident[:, :])
                last.then_inc(kT_psum, 1)

            def project(g, b, i, part, weights):
                if part == 0:
                    project_q(g, b, i, weights)
                elif i < 2:
                    project_kv(g, b, i, weights)
                elif i == 2:
                    transpose_k(g, b)

            def scores(g, b, i):
                if i == 0:
                    pe.wait_ge(kT_split, count(1, g, b, 1))
                    pe.wait_ge(q_split, count(4, g, b, 4))
                width = max(256, P * (i + 1))
                cols = slice(i * P, (i + 1) * P)
                for m, heads in enumerate(SHARE[i]):
                    use = USE0[i] + m
                    wait_count(pe, exps_ok, count(USES, g, b, use - 2))
                    for k, h in enumerate(heads):
                        s = bank[S_BANKS[use % 3]]
                        product(s[:, 256 * k:256 * k + width],
                                [(q_hi[:, b, h, cols], q_lo[:, b, h, cols], kT_hi[:, b, 0:width], kT_lo[:, b, 0:width])],
                                stop=False)
                        diagonal = 256 * k + P * i
                        last = nc.tensor.matmul(s[:, diagonal:diagonal + P], ident16[:, :], causal[:, :],
                                                start=False, stop=True)
                    last.then_inc(s_psum, 1)

            def transpose_p(g, b, i, j):
                n = TR0[i] + j
                if j == 0:
                    pe.wait_ge(prob_ok, count(4, g, b, i + 1))
                wait_count(pe, pT_split, count(TRS, g, b, n - 1))
                for h in range(G):
                    last = nc.tensor.transpose(bank[PT_BANKS[n % 2]][:, h * P:(h + 1) * P],
                                               prob[:, h, j * P:(j + 1) * P], ident[:, :])
                last.then_inc(pT_psum, 1)

            def values(g, b, i, j):
                n = TR0[i] + j
                pe.wait_ge(pT_split, count(TRS, g, b, n + 1))
                if j == 0:
                    wait_count(pe, oT_split, count(4, g, b, i))
                a_hi, a_lo, c_hi, c_lo = v_hi[:, b, j, :], v_lo[:, b, j, :], pT_hi[:, n % 2, :], pT_lo[:, n % 2, :]
                nc.tensor.matmul(bank[OT_BANK][:, :], a_lo, c_hi, start=j == 0, stop=False)
                nc.tensor.matmul(bank[OT_BANK][:, :], a_hi, c_lo, start=False, stop=False)
                nc.tensor.matmul(bank[OT_BANK][:, :], a_hi, c_hi, start=False, stop=j == i).then_inc(pv_done, 1)

            def project_out(pg, pb, pi, wo_of=None):
                if wo_of is not None:
                    pe.wait_ge(wo_split, 4 * wo_of + 4)
                pe.wait_ge(oT_split, count(4, pg, pb, pi + 1))
                wait_count(pe, o_added, count(4, pg, pb, pi))
                product(bank[OUT_BANK][:, :],
                        [(oT_hi[:, pi % 2, h], oT_lo[:, pi % 2, h], wo_hi[:, h, :], wo_lo[:, h, :])
                         for h in range(G)]).then_inc(o_psum, 1)

            pe.wait_ge(down_added, EXPERTS_DONE)
            for i in range(TB):
                project(0, 0, i, 0, True)
                project(0, 0, i, 1, True)

            def step(g, b, more, first=False):
                ng, nb = (g, 1) if b == 0 else (g + 1, 0)
                for i in range(TB):
                    before_this = (g, b, i - 1) if i else (g, 0, TB - 1) if b else (g - 1, 1, TB - 1)
                    any_before = bool(i) or not first
                    scores(g, b, i)
                    if any_before:
                        values(*before_this, before_this[2])
                    if more or b == 0:
                        project(ng, nb, i, 0, b == 1)
                    if any_before:
                        project_out(*before_this, wo_of=g if b == 0 and i == 1 else None)
                    transpose_p(g, b, i, 0)
                    if i:
                        transpose_p(g, b, i, 1)
                    if more or b == 0:
                        project(ng, nb, i, 1, b == 1)
                    for j in range(i):
                        values(g, b, i, j)
                        if j + 2 <= i:
                            transpose_p(g, b, i, j + 2)

            step(0, 0, True, first=True)
            step(0, 1, True)
            with pe.Fori(1, KV - 1) as g:
                step(g, 0, True)
                step(g, 1, True)
            step(KV - 1, 0, False)
            step(KV - 1, 1, False)
            values(KV - 1, 1, TB - 1, TB - 1)
            project_out(KV - 1, 1, TB - 1)


def rotary_tables():
    half = P // 2
    inv = 1.0 / 500000.0 ** (np.arange(0, P, 2, dtype=np.float32) / P)
    wavelen = 2.0 * np.pi / inv
    scaled = np.where(wavelen > 1024.0, inv / 8.0, inv)
    smooth = (1024.0 / wavelen - 1.0) / (4.0 - 1.0)
    smoothed = (1.0 - smooth) / 8.0 * inv + smooth * inv
    medium = (wavelen <= 1024.0) & (wavelen >= 256.0)
    freq = np.where(medium, smoothed, scaled).astype(np.float32)
    angle = np.arange(T, dtype=np.float32)[:, None] * freq[None, :]
    cos, sin = np.cos(angle), np.sin(angle)
    scale = np.float32(1.0 / np.sqrt(P))
    q_cos = np.concatenate([cos.T, cos.T]) * scale
    q_sin = np.concatenate([sin.T, -sin.T]) * scale
    k_rot = np.stack([cos, -sin, sin], axis=1).reshape(TB, P, 3, half).transpose(1, 0, 2, 3)
    return [np.ascontiguousarray(a, dtype=np.float32) for a in (q_cos, q_sin, k_rot)]


def kernel(L0_attn_x, L0_attn_Wq, L0_attn_Wk, L0_attn_Wv, L0_attn_Wo, L0_ffn_router_w, L0_ffn_router_b,
           L0_ffn_router_bias, L0_ffn_ew1, L0_ffn_eb1, L0_ffn_ew2, L0_ffn_eb2, L0_ffn_ew3, L0_ffn_eb3,
           L0_ffn_sw1, L0_ffn_sb1, L0_ffn_sw2, L0_ffn_sb2, L0_ffn_sw3, L0_ffn_sb3):
    import concourse.bacc as bacc
    from concourse.bass_utils import run_bass_kernel_spmd

    def heads(w, n):
        return np.asarray(w).reshape(n, P, HC, P).transpose(0, 3, 2, 1).reshape(n, P, D)

    def halves(w):
        w = np.asarray(w)
        return np.moveaxis(w.reshape(*w.shape[:-1], 2, P), -2, 0)

    def rows(w1):
        return w1.reshape(SLOTS, HC, P, P).transpose(0, 2, 1, 3).reshape(SLOTS, P, D)

    w1 = np.concatenate([np.asarray(L0_ffn_ew1), halves(L0_ffn_sw1)])
    w2 = np.concatenate([np.asarray(L0_ffn_ew2), halves(L0_ffn_sw2)])
    w3 = np.concatenate([np.asarray(L0_ffn_ew3), np.asarray(L0_ffn_sw3).reshape(2, P, D)])
    b1 = np.concatenate([np.asarray(L0_ffn_eb1), halves(L0_ffn_sb1)])
    b2 = np.concatenate([np.asarray(L0_ffn_eb2), halves(L0_ffn_sb2)])
    q_cos, q_sin, k_rot = rotary_tables()
    arrays = {
        "x": np.asarray(L0_attn_x).reshape(B * T, D),
        "wq": heads(L0_attn_Wq, HEADS),
        "wk": heads(L0_attn_Wk, KV),
        "wv": heads(L0_attn_Wv, KV),
        "wo": np.asarray(L0_attn_Wo).T.reshape(HEADS, P, D),
        "experts": np.concatenate([rows(w1), rows(w2), w3, b1[:, :, None], b2[:, :, None]], axis=2),
        "eb3": np.concatenate([np.asarray(L0_ffn_eb3), np.asarray(L0_ffn_sb3)[None]]),
        "router_w": np.asarray(L0_ffn_router_w),
        "router_b": np.asarray(L0_ffn_router_b),
        "router_bias": np.asarray(L0_ffn_router_bias),
        "q_cos": q_cos,
        "q_sin": q_sin,
        "k_rot": k_rot,
    }
    arrays = {k: np.ascontiguousarray(a) for k, a in arrays.items()}
    nc = bacc.Bacc("TRN2", target_bir_lowering=False, num_devices=1)
    args = [nc.dram_tensor(k, a.shape, mybir.dt.from_np(a.dtype), kind="ExternalInput").ap()
            for k, a in arrays.items()]
    result = nc.dram_tensor("result", (B * T, D), F32, kind="ExternalOutput").ap()
    build(nc, *args, result)
    r = run_bass_kernel_spmd(nc, [arrays], core_ids=[0])
    return r.results[0]["result"].reshape(B, T, D)
```

```python
from contextlib import ExitStack

import numpy as np

import concourse.bass as bass
from concourse import mybir

F32 = mybir.dt.float32
F32R = mybir.dt.float32r
BF16 = mybir.dt.bfloat16
ALU = mybir.AluOpType
ACT = mybir.ActivationFunctionType
AX_X = mybir.AxisListType.X

P = 128
B, T, D = 2, 512, 512
TB = T // P
NB = B * TB
HC = D // P
HEADS, KV = 32, 8
G = HEADS // KV
E, GROUPS, TOPG, TOPK = 16, 4, 2, 2
EG = E // GROUPS
SLOTS = E + 2
PAIRS = SLOTS // 2
EPS = 1e-5
BIG = 3.0e38
MASKED = -1.0e38

TR_BANKS, ROUTE_BANK, GATE_BANKS = (5, 6), 7, (4, 5)
LT_BANKS = (3, 4)
UP_BANKS, LIN_BANKS, DOWN_BANKS = (0, 1), (2, 3), (4, 5, 6, 7)
B3_BANKS = UP_BANKS + LIN_BANKS
S_BANKS, PROJ_BANK, OUT_BANK, PT_BANKS, OT_BANK = (0, 1, 2), 3, 4, (5, 6), 7
FIRST_Q_BANKS, FIRST_KV_BANKS, FIRST_KT_BANK = (3, 0, 1, 2), (4, 5), 6

SHARE = [((0, 1), (2, 3)), ((0, 1), (2, 3)), ((0,), (1,), (2,), (3,)), ((0,), (1,), (2,), (3,))]
HALVES = [((0,), (1,)), ((0,), (1,)), ((0, 1), (2, 3)), ((0, 1), (2, 3))]
USES = 12
USE0 = [0, 2, 4, 8]
TRS = 10
TR0 = [0, 1, 3, 6]

Q_SLOT, Q_ORDER = (4, 0, 1, 3), (1, 2, 4, 6)
K_SLOT, K_ORDER, V_SLOT, V_ORDER = 2, 3, 4, 5


def wait_count(eng, sem, value):
    if not isinstance(value, int) or value > 0:
        eng.wait_ge(sem, value)


def count(per_step, g, b, k):
    return (2 * per_step) * g + (per_step * b + k)


def block_before(g, b, i, n=1):
    i -= n
    return (g, b, i) if i >= 0 else (g, 0, i + TB) if b else (g - 1, 1, i + TB)


def build(nc, x, wq, wk, wv, wo, experts, eb3, router_w, router_b, router_bias,
          q_cos, q_sin, k_rot, out):
    gate_rows = nc.dram_tensor("gate_rows", (E, B * T), F32).ap()
    xt = x.rearrange("(n p) d -> n p d", p=P)
    ot = out.rearrange("(n p) d -> n p d", p=P)

    with ExitStack() as ctx:
        def sb(name, shape, dt=F32, stack=ctx):
            return stack.enter_context(nc.sbuf_tensor(name, shape, dt))

        def sem(name):
            return ctx.enter_context(nc.semaphore(name))

        y = sb("y", [P, NB, D])
        xT_hi = sb("xT_hi", [P, HC, B * T], F32R)
        xT_lo = sb("xT_lo", [P, HC, B * T], F32R)
        ident = sb("ident", [P, P])
        ident16 = sb("ident16", [P, P], BF16)
        causal = sb("causal", [P, P], BF16)
        bank = [ctx.enter_context(nc.psum_tensor(f"bank{i}", [P, 512], F32)) for i in range(8)]

        raw = sb("raw", [P, 5, D])
        wq_hi = sb("wq_hi", [P, G, D], F32R)
        wq_lo = sb("wq_lo", [P, G, D], F32R)
        wkv_hi = sb("wkv_hi", [P, HC, 2, P], F32R)
        wkv_lo = sb("wkv_lo", [P, HC, 2, P], F32R)

        early = ExitStack()
        with ExitStack() as stage1:
            xn = sb("xn", [P, NB, D], stack=stage1)
        h_hi = sb("h_hi", [P, 2, B, T], F32R, early)
        h_lo = sb("h_lo", [P, 2, B, T], F32R, early)
        stats = sb("stats", [P, NB, 6], stack=early)
        mv = sb("mv", [P, NB, 2], stack=early)
        lnt = sb("lnt", [P, 4, NB], stack=early)
        rw = sb("rw", [P, HC, E], stack=early)
        rw_hi = sb("rw_hi", [P, HC, E], F32R, early)
        rw_lo = sb("rw_lo", [P, HC, E], F32R, early)
        rb = sb("rb", [P, 2, E], stack=early)
        lT = sb("lT", [E, B * T], stack=early)
        route = sb("route", [P, 3, NB, E], stack=early)
        score, masked, chosen = route[:, 0], route[:, 1], route[:, 2]
        red = sb("red", [P, 3, NB], stack=early)
        grp = sb("grp", [P, 3, NB, GROUPS], stack=early)
        beat = sb("beat", [P, 2, NB, E, E], stack=early)
        before = sb("before", [P, E, E], stack=early)
        gates = sb("gates", [P, NB, P], stack=early)
        gT = sb("gT", [P, B * T], stack=early)
        gT_hi = sb("gT_hi", [P, B * T], F32R, early)
        gT_lo = sb("gT_lo", [P, B * T], F32R, early)
        b3 = sb("b3", [P, D], stack=early)
        b3_hi = sb("b3_hi", [P, D], F32R, early)
        b3_lo = sb("b3_lo", [P, D], F32R, early)
        eraw = sb("eraw", [P, 2, 3 * D + 2], stack=early)
        ew_hi = sb("ew_hi", [P, 2, 3, D], F32R, early)
        ew_lo = sb("ew_lo", [P, 2, 3, D], F32R, early)
        ebias = sb("ebias", [P, 2, 2], stack=early)
        gate = sb("gate", [P, 2, B * T], stack=early)
        act_out = sb("act_out", [P, 2, T], stack=early)
        hid = sb("hid", [P, 2, T], stack=early)
        early.close()

        qc = sb("qc", [P, T])
        qs = sb("qs", [P, T])
        kr = sb("kr", [P, TB, 3, 64])
        wo_hi = sb("wo_hi", [P, G, D], F32R)
        wo_lo = sb("wo_lo", [P, G, D], F32R)
        q_hi = sb("q_hi", [P, B, G, T], F32R)
        q_lo = sb("q_lo", [P, B, G, T], F32R)
        kT_hi = sb("kT_hi", [P, B, T], F32R)
        kT_lo = sb("kT_lo", [P, B, T], F32R)
        v_hi = sb("v_hi", [P, B, TB, P], F32R)
        v_lo = sb("v_lo", [P, B, TB, P], F32R)
        rot = sb("rot", [P, 3, T])
        krot = sb("krot", [P, 2, 2, P])
        ksum = sb("ksum", [P, TB, P])
        prob = sb("prob", [P, 2, G, T])
        pT_hi = sb("pT_hi", [P, 2, G * P], F32R)
        pT_lo = sb("pT_lo", [P, 2, G * P], F32R)
        oT_hi = sb("oT_hi", [P, 2, G, P], F32R)
        oT_lo = sb("oT_lo", [P, 2, G, P], F32R)
        nmax = sb("nmax", [P, TB * G])
        psum_row = sb("psum_row", [P, TB * G])
        rsum = sb("rsum", [P, TB * G])

        x_in = [sem(f"x_in{i}") for i in range(NB)]
        small_in = sem("small_in")
        b3_zero = sem("b3_zero")
        consts = sem("consts")
        chain = sem("chain")
        var_ready, std_ready = sem("var_ready"), sem("std_ready")
        xn_ready, xT_psum, xT_hi_ok, xT_ok = sem("xn_ready"), sem("xT_psum"), sem("xT_hi_ok"), sem("xT_ok")
        lT_psum, lT_copied = sem("lT_psum"), sem("lT_copied")
        rw_ok, logits_ok, shifted_ok, exp_ok = sem("rw_ok"), sem("logits_ok"), sem("shifted_ok"), sem("exp_ok")
        gates_ok, gT_psum, gT_copied, gT_ok = sem("gates_ok"), sem("gT_psum"), sem("gT_copied"), sem("gT_ok")
        gate_stored, b3_psum, b3_added = sem("gate_stored"), sem("b3_psum"), sem("b3_added")
        eraw_in = [sem(f"eraw_in{s}") for s in range(2)]
        gate_in = [sem(f"gate_in{s}") for s in range(2)]
        ones_ok = sem("ones_ok")
        ew_hi_ok, ew_split = sem("ew_hi_ok"), sem("ew_split")
        up_psum, silu_ok, lin_ok, h_ok = sem("up_psum"), sem("silu_ok"), sem("lin_ok"), sem("h_ok")
        h_hi_ok, h_split, down_psum, down_added = sem("h_hi_ok"), sem("h_split"), sem("down_psum"), sem("down_added")
        tables_in = sem("tables_in")
        raw_in = [sem(f"raw_in{s}") for s in range(5)]
        w_hi_ok, w_split, wo_hi_ok, wo_split = sem("w_hi_ok"), sem("w_split"), sem("wo_hi_ok"), sem("wo_split")
        q_psum, q_turned, q_summed, q_hi_ok, q_split = (sem(n) for n in ("q_psum", "q_turned", "q_summed", "q_hi_ok", "q_split"))
        kv_psum, k_turned, k_summed, v_hi_ok, v_split = (sem(n) for n in ("kv_psum", "k_turned", "k_summed", "v_hi_ok", "v_split"))
        kT_psum, kT_hi_ok, kT_split = sem("kT_psum"), sem("kT_hi_ok"), sem("kT_split")
        s_psum, max_ok, exps_ok, rsum_ok, prob_ok = (sem(n) for n in ("s_psum", "max_ok", "exps_ok", "rsum_ok", "prob_ok"))
        pT_psum, pT_hi_ok, pT_split, pv_done = (sem(n) for n in ("pT_psum", "pT_hi_ok", "pT_split", "pv_done"))
        oT_hi_ok, oT_split, o_psum, o_added = (sem(n) for n in ("oT_hi_ok", "oT_split", "o_psum", "o_added"))
        stored = sem("stored")
        pool_free = sem("pool_free")

        block = ctx.enter_context(nc.Block())
        EXPERTS_DONE = NB

        @block.sync
        def _(sp):
            def load(slot, src):
                sp.dma_start(raw[:, slot, :], src).then_inc(raw_in[slot], 16)

            for n in range(NB):
                sp.dma_start(y[:, n, :], xt[n]).then_inc(x_in[n], 16)
            sp.dma_start(rw[:, :, :], router_w.rearrange("(c p) e -> p c e", p=P)).then_inc(small_in, 16)
            sp.dma_start(rb[:, 0, :], router_b.partition_broadcast(P)).then_inc(small_in, 16)
            sp.dma_start(rb[:, 1, :], router_bias.partition_broadcast(P)).then_inc(small_in, 16)
            sp.wait_ge(b3_zero, 1)
            sp.dma_start(b3[0:E + 1, :], eb3).then_inc(small_in, 16)

            for s in range(2):
                sp.dma_start(eraw[:, s, :], experts[s]).then_inc(eraw_in[s], 16)
            sp.wait_ge(gT_copied, 1)
            sp.dma_start(gate_rows, gT[0:E, :]).then_inc(gate_stored, 16)
            sp.wait_ge(gate_stored, 16)
            for h in range(G):
                load(Q_SLOT[h], wq[h])
            load(K_SLOT, wk[0])
            with sp.Fori(1, PAIRS) as q:
                for s in range(2):
                    sp.wait_ge(ew_split, 6 * q + (s - 1))
                    sp.dma_start(eraw[:, s, :], experts[bass.ds(2 * q + s, 1), :, :].rearrange("a p n -> (a p) n"))\
                      .then_inc(eraw_in[s], 16)
                for s in range(2):
                    sp.wait_ge(lin_ok, 4 * q + (s - 1))
                    sp.dma_start(gate[:, s, :], gate_rows[bass.ds(2 * q + (s - 2), 1), :].partition_broadcast(P)
                                 .rearrange("p a t -> p (a t)")).then_inc(gate_in[s], 16)

            sp.wait_ge(w_split, 1)
            load(V_SLOT, wv[0])
            sp.wait_ge(b3_added, EXPERTS_DONE)
            sp.dma_start(qc[:, :], q_cos).then_inc(tables_in, 16)
            sp.dma_start(qs[:, :], q_sin).then_inc(tables_in, 16)
            sp.dma_start(kr[:, :, :, :], k_rot).then_inc(tables_in, 16)

            def key_head(g, more):
                def row(t, n):
                    return t[bass.ds(n, 1), :, :].rearrange("a p n -> (a p) n")
                for c, order in enumerate((Q_ORDER[1], Q_ORDER[2], K_ORDER, Q_ORDER[3])):
                    sp.wait_ge(w_split, 6 * g + order)
                    load(c, row(wo, G * g + c))
                if more:
                    sp.wait_ge(w_split, 6 * g + V_ORDER)
                    load(Q_SLOT[0], row(wq, G * g + G))
                    sp.wait_ge(wo_split, 4 * g + 1)
                    load(Q_SLOT[1], row(wq, G * g + (G + 1)))
                    sp.wait_ge(wo_split, 4 * g + 3)
                    load(Q_SLOT[2], row(wq, G * g + (G + 2)))
                    load(K_SLOT, row(wk, g + 1))
                    sp.wait_ge(wo_split, 4 * g + 4)
                    load(Q_SLOT[3], row(wq, G * g + (G + 3)))
                    sp.wait_ge(w_split, 6 * g + (6 + Q_ORDER[0]))
                    load(V_SLOT, row(wv, g + 1))

            with sp.Fori(0, KV - 1) as g:
                key_head(g, True)
            key_head(KV - 1, False)

            for n in range(NB):
                sp.wait_ge(o_added, 8 * (KV - 1) + n + 1)
                sp.dma_start(ot[n], y[:, n, :]).then_inc(stored, 16)
            sp.wait_ge(stored, 16 * NB)

        @block.gpsimd
        def _(pool):
            nc.gpsimd.memset(ident[:, :], 0.0).then_inc(consts, 1)
            nc.gpsimd.memset(ident16[:, :], 0.0).then_inc(consts, 1)
            nc.gpsimd.memset(causal[:, :], 0.0).then_inc(consts, 1)
            nc.gpsimd.memset(before[:, :, :], 1.0).then_inc(consts, 1)
            pool.wait_ge(consts, 4)
            for m in (ident, ident16):
                nc.gpsimd.affine_select(out=m[:, :], in_=m[:, :], compare_op=ALU.not_equal, fill=1.0, base=0,
                                        pattern=[[-1, P]], channel_multiplier=1).then_inc(consts, 1)
            nc.gpsimd.affine_select(out=causal[:, :], in_=causal[:, :], compare_op=ALU.is_ge, fill=MASKED, base=0,
                                    pattern=[[-1, P]], channel_multiplier=1).then_inc(consts, 1)
            nc.gpsimd.affine_select(out=before[:, :, :], in_=before[:, :, :], compare_op=ALU.is_gt, fill=0.0, base=0,
                                    pattern=[[1, E], [-1, E]], channel_multiplier=0).then_inc(consts, 1)

            nc.gpsimd.memset(gate[:, :, :], 1.0).then_inc(ones_ok, 1)

            def split(hi, lo, src, hi_ok, lo_ok, n):
                nc.gpsimd.tensor_scalar(hi, src, 1.0, 1.0, ALU.mult, ALU.mult).then_inc(hi_ok, 1)
                pool.wait_ge(hi_ok, n)
                nc.gpsimd.tensor_tensor(lo, src, hi.bitcast(F32), ALU.subtract).then_inc(lo_ok, 1)

            def expert_weights(q):
                for s in range(2):
                    pool.wait_ge(eraw_in[s], 16 * q + 16)
                    wait_count(pool, up_psum, 4 * q + (s - 1))
                    wait_count(pool, silu_ok, 4 * q + (s - 1))
                    wait_count(pool, lin_ok, 4 * q + (s - 1))
                    pool.sem_inc(pool_free, 1)
                    nc.gpsimd.tensor_copy(ebias[:, s, :], eraw[:, s, 3 * D:3 * D + 2])
                    for m in range(2):
                        split(ew_hi[:, s, m, :], ew_lo[:, s, m, :], eraw[:, s, m * D:(m + 1) * D],
                              ew_hi_ok, ew_split, 6 * q + (2 * s + m + 1))
                for s in range(2):
                    wait_count(pool, down_psum, 8 * q)
                    pool.sem_inc(pool_free, 1)
                    split(ew_hi[:, s, 2, :], ew_lo[:, s, 2, :], eraw[:, s, 2 * D:3 * D],
                          ew_hi_ok, ew_split, 6 * q + (5 + s))

            expert_weights(0)
            with pool.Fori(1, PAIRS) as q:
                expert_weights(q)

            def add_q(g, b, h):
                pool.wait_ge(q_turned, count(4, g, b, h + 1))
                wait_count(pool, q_split, count(4, g, b, h))
                nc.gpsimd.tensor_tensor(rot[:, 2, :], rot[:, 0, :], rot[:, 1, :], ALU.add).then_inc(q_summed, 1)

            def add_k(g, b, i):
                pool.wait_ge(k_turned, count(2, g, b, i + 1))
                nc.gpsimd.tensor_tensor(ksum[:, 2 * i:2 * i + 2, :], krot[:, 0], krot[:, 1], ALU.add)\
                    .then_inc(k_summed, 1)

            def split_q(g, h, used):
                wait_count(pool, q_psum, used)
                pool.wait_ge(raw_in[Q_SLOT[h]], 32 * g + 16)
                pool.sem_inc(pool_free, 1)
                split(wq_hi[:, h, :], wq_lo[:, h, :], raw[:, Q_SLOT[h], :], w_hi_ok, w_split, 6 * g + Q_ORDER[h])

            def split_kv(g, kv, used):
                slot, order = ((K_SLOT, K_ORDER), (V_SLOT, V_ORDER))[kv]
                wait_count(pool, kv_psum, used)
                pool.wait_ge(raw_in[slot], 32 * g + (16, 32)[kv])
                pool.sem_inc(pool_free, 1)
                src = raw[:, slot, :].rearrange("p (c o) -> p c o", c=HC)
                split(wkv_hi[:, :, kv, :], wkv_lo[:, :, kv, :], src, w_hi_ok, w_split, 6 * g + order)

            def normalise(g, b, i):
                pool.wait_ge(rsum_ok, count(4, g, b, i + 1))
                pool.sem_inc(pool_free, 1)
                for h in range(G):
                    row = prob[:, i % 2, h, 0:P * (i + 1)]
                    last = nc.gpsimd.tensor_scalar(row, row, rsum[:, G * i + h:G * i + h + 1], 1.0, ALU.mult, ALU.mult)
                last.then_inc(prob_ok, 1)

            split_q(0, 0, 0)
            split_q(0, 1, 0)
            split_kv(0, 0, 0)
            split_q(0, 2, 0)
            split_kv(0, 1, 0)
            split_q(0, 3, 0)
            add_k(0, 0, 0)
            add_q(0, 0, 0)
            add_k(0, 0, 1)
            add_q(0, 0, 1)
            add_q(0, 0, 2)
            add_q(0, 0, 3)

            def step(g, b, more):
                ng, nb = (g, 1) if b == 0 else (g + 1, 0)
                feeds = more or b == 0
                for i in range(TB):
                    if feeds and i:
                        add_q(ng, nb, i - 1)
                    normalise(g, b, i)
                    if feeds and i < 2:
                        add_k(ng, nb, i)
                    if feeds and i == TB - 1:
                        add_q(ng, nb, i)
                    if more:
                        if (b, i) == (0, 1):
                            split_q(g + 1, 0, count(4, g, 1, 1))
                        if (b, i) == (0, 2):
                            split_q(g + 1, 1, count(4, g, 1, 2))
                            split_kv(g + 1, 0, count(2, g, 1, 2))
                        if (b, i) == (0, 3):
                            split_q(g + 1, 2, count(4, g, 1, 3))
                            split_kv(g + 1, 1, count(2, g, 1, 2))
                        if (b, i) == (1, 0):
                            split_q(g + 1, 3, count(4, g, 1, 4))

            with pool.Fori(0, KV - 1) as g:
                step(g, 0, True)
                step(g, 1, True)
            step(KV - 1, 0, False)
            step(KV - 1, 1, False)

        @block.scalar
        def _(act):
            act.wait_ge(var_ready, 1)
            nc.scalar.activation(lnt[:, 1, :], lnt[:, 0, :], ACT.Sqrt).then_inc(std_ready, 1)
            for n in range(B * HC):
                c, b = n % HC, n // HC
                act.wait_ge(xT_psum, n + 1)
                nc.scalar.activation(xT_hi[:, c, b * T:(b + 1) * T], bank[TR_BANKS[n % 2]][:, :], ACT.Copy)\
                    .then_inc(xT_hi_ok, 1)
            act.wait_ge(lT_psum, 1)
            for j in range(B):
                last = nc.scalar.activation(lT[:, j * T:(j + 1) * T], bank[LT_BANKS[j]][0:E, :], ACT.Copy)
            last.then_inc(lT_copied, 1)
            act.wait_ge(shifted_ok, 1)
            nc.scalar.activation(score, score, ACT.Exp).then_inc(exp_ok, 1)

            def gates_in_rows():
                act.wait_ge(gT_psum, 1)
                for j in range(2):
                    last = nc.scalar.activation(gT[:, j * T:(j + 1) * T], bank[GATE_BANKS[j]][:, :], ACT.Copy)
                last.then_inc(gT_copied, 1)

            def pair(q):
                for t in range(4):
                    s, b = t % 2, t // 2
                    act.wait_ge(up_psum, 4 * q + (t + 1))
                    wait_count(act, h_ok, 4 * q + (t - 1))
                    nc.scalar.activation(act_out[:, t % 2, :], bank[UP_BANKS[t % 2]][:, :], ACT.Silu,
                                         bias=ebias[:, s, 0:1]).then_inc(silu_ok, 1)
                    act.wait_ge(h_ok, 4 * q + (t + 1))
                    nc.scalar.activation(h_hi[:, s, b, :], hid[:, t % 2, :], ACT.Copy).then_inc(h_hi_ok, 1)

            pair(0)
            gates_in_rows()
            with act.Fori(1, PAIRS) as q:
                pair(q)

            act.wait_ge(b3_added, EXPERTS_DONE)

            def hi_q(g, b, h):
                act.wait_ge(q_summed, count(4, g, b, h + 1))
                nc.scalar.activation(q_hi[:, b, h, :], rot[:, 2, :], ACT.Copy).then_inc(q_hi_ok, 1)

            def hi_v(g, b, i, at=PROJ_BANK):
                act.wait_ge(k_turned, count(2, g, b, i + 1))
                if i == 0:
                    wait_count(act, pv_done, count(TRS, g, b, TR0[TB - 1] + 2 - 2 * TRS))
                src = bank[at].rearrange("p (n k o) -> p n k o", n=2, k=2)[:, :, 1, :]
                nc.scalar.activation(v_hi[:, b, 2 * i:2 * i + 2, :], src, ACT.Copy).then_inc(v_hi_ok, 1)

            def hi_kT(g, b, at=PROJ_BANK):
                act.wait_ge(kT_psum, count(1, g, b, 1))
                nc.scalar.activation(kT_hi[:, b, :], bank[at][:, :], ACT.Copy).then_inc(kT_hi_ok, 1)

            def exps(g, b, i, m):
                use = USE0[i] + m
                act.wait_ge(max_ok, count(USES, g, b, use + 1))
                for k, h in enumerate(SHARE[i][m]):
                    col = slice(G * i + h, G * i + h + 1)
                    last = nc.scalar.activation(prob[:, i % 2, h, 0:P * (i + 1)],
                                                bank[S_BANKS[use % 3]][:, 256 * k:256 * k + P * (i + 1)], ACT.Exp,
                                                bias=nmax[:, col], accum_out=psum_row[:, col])
                last.then_inc(exps_ok, 1)

            def hi_oT(pg, pb, pi):
                act.wait_ge(pv_done, count(TRS, pg, pb, TR0[pi] + pi + 1))
                wait_count(act, o_psum, count(4, pg, pb, pi - 1))
                nc.scalar.activation(oT_hi[:, pi % 2], bank[OT_BANK].rearrange("p (h t) -> p h t", h=G), ACT.Copy)\
                    .then_inc(oT_hi_ok, 1)

            def hi_pT(g, b, n):
                act.wait_ge(pT_psum, count(TRS, g, b, n + 1))
                wait_count(act, pv_done, count(TRS, g, b, n - 1))
                nc.scalar.activation(pT_hi[:, n % 2, :], bank[PT_BANKS[n % 2]][:, :], ACT.Copy).then_inc(pT_hi_ok, 1)

            hi_v(0, 0, 0, FIRST_KV_BANKS[0])
            hi_q(0, 0, 0)
            hi_v(0, 0, 1, FIRST_KV_BANKS[1])
            hi_q(0, 0, 1)
            hi_kT(0, 0, FIRST_KT_BANK)
            hi_q(0, 0, 2)
            hi_q(0, 0, 3)

            def slot(g, b, i, more, begun):
                following = (g, 1) if b == 0 else (g + 1, 0)
                feeds = more or b == 0
                last = block_before(g, b, i)
                values = [last[:2] + (TR0[last[2]] + j,) for j in range(last[2] + 1)] if begun else []
                if i == 0 and begun:
                    hi_q(g, b, TB - 1)
                for part in HALVES[i][0]:
                    exps(g, b, i, part)
                for v in values[:2]:
                    hi_pT(*v)
                for part in HALVES[i][1]:
                    exps(g, b, i, part)
                if feeds and i:
                    hi_q(*following, i - 1)
                for v in values[2:]:
                    hi_pT(*v)
                if feeds and i < 2:
                    hi_v(*following, i)
                if feeds and i == 2:
                    hi_kT(*following)
                if begun:
                    hi_oT(*last)
                if b == 0 and i == 1:
                    wait_count(act, o_psum, 8 * g)
                    for c in range(G):
                        act.wait_ge(raw_in[c], 32 * g + 32)
                        nc.scalar.activation(wo_hi[:, c, :], raw[:, c, :], ACT.Copy).then_inc(wo_hi_ok, 1)

            def key_head(g, more, first=False):
                for n in range(B * TB):
                    slot(g, n // TB, n % TB, more, n > 0 or not first)

            key_head(0, True, first=True)
            with act.Fori(1, KV - 1) as g:
                key_head(g, True)
            key_head(KV - 1, False)
            for j in range(TB):
                hi_pT(KV - 1, 1, TR0[TB - 1] + j)
            hi_oT(KV - 1, 1, TB - 1)

        @block.vector
        def _(dve):
            done = [0]

            def link(ins):
                done[0] += 1
                ins.then_inc(chain, 1)
                dve.wait_ge(chain, done[0])

            nc.vector.memset(b3[:, :], 0.0).then_inc(b3_zero, 1)
            link(nc.vector.memset(gates[:, :, :], 0.0))
            link(nc.vector.memset(gates[:, :, E:SLOTS], 1.0))
            for n in range(NB):
                dve.wait_ge(x_in[n], 16)
                last = nc.vector.bn_stats(stats[:, n, :], y[:, n, :])
            link(last)
            for n in range(NB):
                last = nc.vector.bn_aggr(mv[:, n, :], stats[:, n, :])
            link(last)
            var, std, inv, tmp = (lnt[:, k, :] for k in range(4))
            nc.vector.tensor_scalar(var, mv[:, :, 1], EPS, None, ALU.add).then_inc(var_ready, 1)
            dve.wait_ge(std_ready, 1)
            link(nc.vector.reciprocal(inv, std))
            link(nc.vector.tensor_tensor(tmp, inv, inv, ALU.mult))
            link(nc.vector.tensor_tensor(tmp, tmp, var, ALU.mult))
            link(nc.vector.tensor_scalar(tmp, tmp, -0.5, 1.5, ALU.mult, ALU.add))
            link(nc.vector.tensor_tensor(inv, inv, tmp, ALU.mult))
            for n in range(NB):
                nc.vector.tensor_scalar(xn[:, n, :], y[:, n, :], mv[:, n, 0:1], inv[:, n:n + 1],
                                        ALU.subtract, ALU.mult).then_inc(xn_ready, 1)
            dve.wait_ge(small_in, 64)
            link(nc.vector.tensor_copy(rw_hi[:, :, :], rw[:, :, :]))
            nc.vector.tensor_tensor(rw_lo[:, :, :], rw[:, :, :], rw_hi[:, :, :].bitcast(F32), ALU.subtract)\
                .then_inc(rw_ok, 1)
            link(nc.vector.tensor_copy(b3_hi[:, :], b3[:, :]))
            link(nc.vector.tensor_tensor(b3_lo[:, :], b3[:, :], b3_hi[:, :].bitcast(F32), ALU.subtract))
            for n in range(B * HC):
                c, b = n % HC, n // HC
                span = slice(b * T, (b + 1) * T)
                dve.wait_ge(xT_hi_ok, n + 1)
                nc.vector.tensor_tensor(xT_lo[:, c, span], bank[TR_BANKS[n % 2]][:, :], xT_hi[:, c, span].bitcast(F32),
                                        ALU.subtract).then_inc(xT_ok, 1)

            def hidden(q, t):
                s, b = t % 2, t // 2
                h = hid[:, t % 2, :]
                dve.wait_ge(up_psum, 4 * q + (t + 1))
                if b == 0:
                    if isinstance(q, int):
                        dve.wait_ge(ones_ok, 1)
                    else:
                        dve.wait_ge(gate_in[s], 16 * q)
                nc.vector.scalar_tensor_tensor(h, bank[LIN_BANKS[t % 2]][:, :], ebias[:, s, 1:2],
                                               gate[:, s, b * T:(b + 1) * T], ALU.add, ALU.mult).then_inc(lin_ok, 1)
                dve.wait_ge(lin_ok, 4 * q + (t + 1))
                dve.wait_ge(silu_ok, 4 * q + (t + 1))
                nc.vector.tensor_tensor(h, h, act_out[:, t % 2, :], ALU.mult).then_inc(h_ok, 1)
                dve.wait_ge(h_hi_ok, 4 * q + (t + 1))
                nc.vector.tensor_tensor(h_lo[:, s, b, :], h, h_hi[:, s, b, :].bitcast(F32), ALU.subtract)\
                    .then_inc(h_split, 1)

            def over_blocks(row):
                return row.unsqueeze(1).broadcast_to([P, NB, E])

            def over_experts(col):
                return col.unsqueeze(2).broadcast_to([P, NB, E])

            dve.wait_ge(logits_ok, 1)
            logits = bank[ROUTE_BANK][:, 0:NB * E].rearrange("p (n e) -> p n e", n=NB)
            link(nc.vector.tensor_tensor(score, logits, over_blocks(rb[:, 0, :]), ALU.add))
            link(nc.vector.tensor_reduce(red[:, 0, :], score, AX_X, ALU.max))
            nc.vector.tensor_tensor(score, score, over_experts(red[:, 0, :]), ALU.subtract).then_inc(shifted_ok, 1)
            dve.wait_ge(exp_ok, 1)
            link(nc.vector.tensor_reduce(red[:, 1, :], score, AX_X, ALU.add))
            link(nc.vector.reciprocal(red[:, 2, :], red[:, 1, :]))
            link(nc.vector.tensor_tensor(score, score, over_experts(red[:, 2, :]), ALU.mult))
            link(nc.vector.tensor_tensor(score, score, over_blocks(rb[:, 1, :]), ALU.add))

            def top(result, v, n, k, between=lambda t: None):
                v_i = v.unsqueeze(3).broadcast_to([P, NB, n, n])
                v_j = v.unsqueeze(2).broadcast_to([P, NB, n, n])
                more, same = beat[:, 0, :, 0:n, 0:n], beat[:, 1, :, 0:n, 0:n]
                link(nc.vector.tensor_tensor(more, v_j, v_i, ALU.is_gt))
                link(nc.vector.tensor_tensor(same, v_j, v_i, ALU.is_equal))
                between(1)
                link(nc.vector.tensor_tensor(same, same, before[:, 0:n, 0:n].unsqueeze(1).broadcast_to([P, NB, n, n]),
                                             ALU.mult))
                link(nc.vector.tensor_tensor(more, more, same, ALU.add))
                between(2)
                link(nc.vector.tensor_reduce(result, more, AX_X, ALU.add))
                link(nc.vector.tensor_scalar(result, result, float(k), None, ALU.is_lt))

            dve.wait_ge(consts, 8)
            in_groups = score.rearrange("p n (g e) -> p n g e", g=GROUPS)
            link(nc.vector.tensor_reduce(grp[:, 0], in_groups, AX_X, ALU.max))
            top(grp[:, 1], grp[:, 0], GROUPS, TOPG)
            link(nc.vector.tensor_scalar(grp[:, 2], grp[:, 1], -1.0, BIG, ALU.add, ALU.mult))
            masked_groups = masked.rearrange("p n (g e) -> p n g e", g=GROUPS)
            link(nc.vector.tensor_tensor(masked_groups, in_groups,
                                         grp[:, 1].unsqueeze(3).broadcast_to([P, NB, GROUPS, EG]), ALU.mult))
            link(nc.vector.tensor_tensor(masked_groups, masked_groups,
                                         grp[:, 2].unsqueeze(3).broadcast_to([P, NB, GROUPS, EG]), ALU.add))
            hidden(0, 0)
            top(chosen, masked, E, TOPK, between=lambda t: hidden(0, t))
            nc.vector.tensor_tensor(gates[:, :, 0:E], score, chosen, ALU.mult).then_inc(gates_ok, 1)

            def add_down(q, b):
                for k in range(TB):
                    n = TB * b + k
                    dve.wait_ge(down_psum, 8 * q + (n + 1))
                    nc.vector.tensor_tensor(y[:, n, :], y[:, n, :], bank[DOWN_BANKS[n % 4]][:, :], ALU.add)\
                        .then_inc(down_added, 1)

            hidden(0, 3)
            add_down(0, 0)
            with dve.Fori(1, PAIRS) as q:
                hidden(q, 0)
                hidden(q, 1)
                add_down(q - 1, 1)
                hidden(q, 2)
                hidden(q, 3)
                add_down(q, 0)
            link(nc.vector.tensor_copy(gT_hi[:, :], gT[:, :]))
            nc.vector.tensor_tensor(gT_lo[:, :], gT[:, :], gT_hi[:, :].bitcast(F32), ALU.subtract).then_inc(gT_ok, 1)
            add_down(PAIRS - 1, 1)
            for n in range(NB):
                dve.wait_ge(b3_psum, n + 1)
                nc.vector.tensor_tensor(y[:, n, :], y[:, n, :], bank[B3_BANKS[n % 4]][:, :], ALU.add)\
                    .then_inc(b3_added, 1)

            dve.wait_ge(tables_in, 48)

            def turn_q(g, b, h, at=PROJ_BANK, between=lambda: None):
                q = bank[at]
                dve.wait_ge(q_psum, count(4, g, b, h + 1))
                wait_count(dve, q_summed, count(4, g, b, h))
                nc.vector.tensor_tensor(rot[:, 0, :], q[:, :], qc[:, :], ALU.mult)
                between()
                nc.vector.tensor_tensor(rot[0:64, 1, :], q[64:128, :], qs[64:128, :], ALU.mult)
                nc.vector.tensor_tensor(rot[64:128, 1, :], q[0:64, :], qs[0:64, :], ALU.mult).then_inc(q_turned, 1)

            def lo_q(g, b, h):
                dve.wait_ge(q_hi_ok, count(4, g, b, h + 1))
                nc.vector.tensor_tensor(q_lo[:, b, h, :], rot[:, 2, :], q_hi[:, b, h, :].bitcast(F32), ALU.subtract)\
                    .then_inc(q_split, 1)

            def turn_k(g, b, i, at=PROJ_BANK):
                k = bank[at].rearrange("p (n k f o) -> p n k f o", n=2, k=2, f=2)[:, :, 0]
                table = kr[:, 2 * i:2 * i + 2]
                one, two = (krot[:, m].rearrange("p n (f o) -> p n f o", f=2) for m in range(2))
                dve.wait_ge(kv_psum, count(2, g, b, i + 1))
                wait_count(dve, k_summed, count(2, g, b, i))
                nc.vector.tensor_tensor(one, k, table[:, :, 0:1, :].broadcast_to([P, 2, 2, 64]), ALU.mult)
                nc.vector.tensor_tensor(two[:, :, 0, :], k[:, :, 1, :], table[:, :, 1, :], ALU.mult)
                nc.vector.tensor_tensor(two[:, :, 1, :], k[:, :, 0, :], table[:, :, 2, :], ALU.mult)\
                    .then_inc(k_turned, 1)

            def lo_v(g, b, i, at=PROJ_BANK):
                src = bank[at].rearrange("p (n k o) -> p n k o", n=2, k=2)[:, :, 1, :]
                dve.wait_ge(v_hi_ok, count(2, g, b, i + 1))
                nc.vector.tensor_tensor(v_lo[:, b, 2 * i:2 * i + 2, :], src, v_hi[:, b, 2 * i:2 * i + 2, :].bitcast(F32),
                                        ALU.subtract).then_inc(v_split, 1)

            def lo_kT(g, b, at=PROJ_BANK):
                dve.wait_ge(kT_hi_ok, count(1, g, b, 1))
                nc.vector.tensor_tensor(kT_lo[:, b, :], bank[at][:, :], kT_hi[:, b, :].bitcast(F32),
                                        ALU.subtract).then_inc(kT_split, 1)

            def maxima(g, b, i, m):
                heads = SHARE[i][m]
                use, k = USE0[i] + m, len(heads)
                s = bank[S_BANKS[use % 3]][:, :].rearrange("p (k s) -> p k s", k=k)[:, :, 0:P * (i + 1)]
                dve.wait_ge(s_psum, count(USES, g, b, use + 1))
                col = G * i + heads[0]
                nc.vector.tensor_reduce(nmax[:, col:col + k], s, AX_X, ALU.max, negate=True).then_inc(max_ok, 1)

            def inverse_sums(g, b, i):
                dve.wait_ge(exps_ok, count(USES, g, b, USE0[i] + len(SHARE[i])))
                nc.vector.reciprocal(rsum[:, G * i:G * i + G], psum_row[:, G * i:G * i + G]).then_inc(rsum_ok, 1)

            def lo_oT(pg, pb, pi):
                dve.wait_ge(oT_hi_ok, count(4, pg, pb, pi + 1))
                nc.vector.tensor_tensor(oT_lo[:, pi % 2], bank[OT_BANK].rearrange("p (h t) -> p h t", h=G),
                                        oT_hi[:, pi % 2].bitcast(F32), ALU.subtract).then_inc(oT_split, 1)

            def add_out(pg, pb, pi):
                dve.wait_ge(o_psum, count(4, pg, pb, pi + 1))
                n = TB * pb + pi
                nc.vector.tensor_tensor(y[:, n, :], y[:, n, :], bank[OUT_BANK][:, :], ALU.add).then_inc(o_added, 1)

            def lo_pT(g, b, n):
                dve.wait_ge(pT_hi_ok, count(TRS, g, b, n + 1))
                nc.vector.tensor_tensor(pT_lo[:, n % 2, :], bank[PT_BANKS[n % 2]][:, :],
                                        pT_hi[:, n % 2, :].bitcast(F32), ALU.subtract).then_inc(pT_split, 1)

            turn_k(0, 0, 0, FIRST_KV_BANKS[0])
            turn_q(0, 0, 0, FIRST_Q_BANKS[0])
            lo_v(0, 0, 0, FIRST_KV_BANKS[0])
            turn_k(0, 0, 1, FIRST_KV_BANKS[1])
            lo_q(0, 0, 0)
            turn_q(0, 0, 1, FIRST_Q_BANKS[1])
            lo_v(0, 0, 1, FIRST_KV_BANKS[1])
            lo_q(0, 0, 1)
            turn_q(0, 0, 2, FIRST_Q_BANKS[2])
            lo_kT(0, 0, FIRST_KT_BANK)
            lo_q(0, 0, 2)
            turn_q(0, 0, 3, FIRST_Q_BANKS[3])
            lo_q(0, 0, 3)

            def slot(g, b, i, more, begun, begun2):
                following = (g, 1) if b == 0 else (g + 1, 0)
                feeds = more or b == 0
                last = block_before(g, b, i)
                values = [last[:2] + (TR0[last[2]] + j,) for j in range(last[2] + 1)] if begun else []
                ahead = list(HALVES[i][0])
                if feeds and i:
                    if i == 1:
                        turn_q(*following, i - 1)
                    else:
                        turn_q(*following, i - 1, between=lambda: maxima(g, b, i, ahead.pop(0)))
                if i == 0 and begun:
                    lo_q(g, b, TB - 1)
                for part in ahead:
                    maxima(g, b, i, part)
                for v in values[:2]:
                    lo_pT(*v)
                for part in HALVES[i][1]:
                    maxima(g, b, i, part)
                if feeds and i:
                    lo_q(*following, i - 1)
                for v in values[2:3]:
                    lo_pT(*v)
                if feeds and i < 2:
                    turn_k(*following, i)
                for v in values[3:]:
                    lo_pT(*v)
                inverse_sums(g, b, i)
                if feeds and i < 2:
                    lo_v(*following, i)
                if feeds and i == 2:
                    lo_kT(*following)
                if begun:
                    lo_oT(*last)
                if feeds and i == 3:
                    turn_q(*following, i)
                if begun2:
                    add_out(*block_before(g, b, i, 2))
                if b == 0 and i == 1:
                    for c in range(G):
                        dve.wait_ge(wo_hi_ok, 4 * g + (c + 1))
                        nc.vector.tensor_tensor(wo_lo[:, c, :], raw[:, c, :], wo_hi[:, c, :].bitcast(F32),
                                                ALU.subtract).then_inc(wo_split, 1)

            def key_head(g, more, first=False):
                for n in range(B * TB):
                    slot(g, n // TB, n % TB, more, n > 0 or not first, n > 1 or not first)

            key_head(0, True, first=True)
            with dve.Fori(1, KV - 1) as g:
                key_head(g, True)
            key_head(KV - 1, False)
            for j in range(TB):
                lo_pT(KV - 1, 1, TR0[TB - 1] + j)
            add_out(KV - 1, 1, TB - 2)
            lo_oT(KV - 1, 1, TB - 1)
            add_out(KV - 1, 1, TB - 1)

        @block.tensor
        def _(pe):
            def product(dst, terms, stop=True):
                for k, (a_hi, a_lo, c_hi, c_lo) in enumerate(terms):
                    nc.tensor.matmul(dst, a_lo, c_hi, start=k == 0, stop=False)
                    nc.tensor.matmul(dst, a_hi, c_lo, start=False, stop=False)
                    last = nc.tensor.matmul(dst, a_hi, c_hi, start=False, stop=stop and k == len(terms) - 1)
                return last

            pe.wait_ge(consts, 8)
            for n in range(B * HC):
                c, b = n % HC, n // HC
                pe.wait_ge(xn_ready, TB * (b + 1))
                wait_count(pe, xT_ok, n - 1)
                for k in range(TB):
                    last = nc.tensor.transpose(bank[TR_BANKS[n % 2]][:, k * P:(k + 1) * P],
                                               xn[:, TB * b + k, c * P:(c + 1) * P], ident[:, :])
                last.then_inc(xT_psum, 1)
            pe.wait_ge(rw_ok, 1)
            pe.wait_ge(xT_ok, B * HC)
            for b in range(B):
                span = slice(b * T, (b + 1) * T)
                last = product(bank[LT_BANKS[b]][0:E, :],
                               [(rw_hi[:, c, :], rw_lo[:, c, :], xT_hi[:, c, span], xT_lo[:, c, span])
                                for c in range(HC)])
            last.then_inc(lT_psum, 1)

            def logits_by_token():
                pe.wait_ge(lT_copied, 1)
                for n in range(NB):
                    last = nc.tensor.transpose(bank[ROUTE_BANK][:, n * E:(n + 1) * E], lT[:, n * P:(n + 1) * P],
                                               ident[0:E, 0:E])
                last.then_inc(logits_ok, 1)

            def gates_in_rows():
                pe.wait_ge(gates_ok, 1)
                for n in range(NB):
                    last = nc.tensor.transpose(bank[GATE_BANKS[n // TB]][:, n % TB * P:(n % TB + 1) * P],
                                               gates[:, n, :], ident[:, :])
                last.then_inc(gT_psum, 1)

            def output_biases():
                pe.wait_ge(gT_ok, 1)
                pe.wait_ge(silu_ok, 4 * PAIRS)
                pe.wait_ge(lin_ok, 4 * PAIRS)
                for n in range(NB):
                    cols = slice(n * P, (n + 1) * P)
                    wait_count(pe, b3_added, n - 3)
                    product(bank[B3_BANKS[n % 4]][:, :],
                            [(gT_hi[:, cols], gT_lo[:, cols], b3_hi[:, :], b3_lo[:, :])]).then_inc(b3_psum, 1)

            def up(q, t):
                s, b = t % 2, t // 2
                span = slice(b * T, (b + 1) * T)
                if b == 0:
                    pe.wait_ge(ew_split, 6 * q + (2 + 2 * s))
                wait_count(pe, silu_ok, 4 * q + (t - 1))
                wait_count(pe, lin_ok, 4 * q + (t - 1))
                for m, banks in enumerate((UP_BANKS, LIN_BANKS)):
                    last = product(bank[banks[t % 2]][:, :],
                                   [(ew_hi[:, s, m, c * P:(c + 1) * P], ew_lo[:, s, m, c * P:(c + 1) * P],
                                     xT_hi[:, c, span], xT_lo[:, c, span]) for c in range(HC)])
                last.then_inc(up_psum, 1)

            def down(q, b):
                pe.wait_ge(h_split, 4 * q + (2 * b + 2))
                if b == 0:
                    pe.wait_ge(ew_split, 6 * q + 6)
                for k in range(TB):
                    n = TB * b + k
                    wait_count(pe, down_added, 8 * q + (n - 3))
                    cols = slice(k * P, (k + 1) * P)
                    product(bank[DOWN_BANKS[n % 4]][:, :],
                            [(h_hi[:, s, b, cols], h_lo[:, s, b, cols], ew_hi[:, s, 2, :], ew_lo[:, s, 2, :])
                             for s in range(2)]).then_inc(down_psum, 1)

            up(0, 0)
            logits_by_token()
            pe.wait_ge(lT_copied, 1)
            up(0, 1)
            up(0, 2)
            up(0, 3)
            gates_in_rows()
            pe.wait_ge(gT_copied, 1)
            down(0, 0)
            with pe.Fori(1, PAIRS) as q:
                up(q, 0)
                up(q, 1)
                down(q - 1, 1)
                up(q, 2)
                up(q, 3)
                down(q, 0)
            down(PAIRS - 1, 1)
            output_biases()

            def project_q(g, b, h, c, weights, at=None):
                span = slice(b * T, (b + 1) * T)
                if c == 0 and weights:
                    pe.wait_ge(w_split, 6 * g + Q_ORDER[h])
                if c == 0 and at is None:
                    if h < 2:
                        pe.wait_ge(v_split, count(2, g, b, h + 1))
                    elif h == 2:
                        pe.wait_ge(kT_split, count(1, g, b, 1))
                    else:
                        pe.wait_ge(q_turned, count(4, g, b, 3))
                q, col = bank[PROJ_BANK if at is None else at][:, :], slice(c * P, (c + 1) * P)
                nc.tensor.matmul(q, wq_lo[:, h, col], xT_hi[:, c, span], start=c == 0, stop=False)
                nc.tensor.matmul(q, wq_hi[:, h, col], xT_lo[:, c, span], start=False, stop=False)
                last = nc.tensor.matmul(q, wq_hi[:, h, col], xT_hi[:, c, span], start=False, stop=c == HC - 1)
                if c == HC - 1:
                    last.then_inc(q_psum, 1)

            def project_kv(g, b, i, k, weights, at=None):
                if weights and k == 0:
                    pe.wait_ge(w_split, 6 * g + V_ORDER)
                if at is None and k == 0:
                    pe.wait_ge(q_turned, count(4, g, b, i))
                n = TB * b + 2 * i + k
                cols = slice(n * P, (n + 1) * P)
                last = product(bank[PROJ_BANK if at is None else at][:, k * 2 * P:(k + 1) * 2 * P],
                               [(xT_hi[:, c, cols], xT_lo[:, c, cols],
                                 wkv_hi[:, c].rearrange("p k o -> p (k o)"),
                                 wkv_lo[:, c].rearrange("p k o -> p (k o)")) for c in range(HC)])
                if k == 1:
                    last.then_inc(kv_psum, 1)

            def transpose_k(g, b, at=None):
                if at is None:
                    pe.wait_ge(q_turned, count(4, g, b, 2))
                pe.wait_ge(k_summed, count(2, g, b, 2))
                for k in range(TB):
                    last = nc.tensor.transpose(bank[PROJ_BANK if at is None else at][:, k * P:(k + 1) * P], ksum[:, k, :], ident[:, :])
                last.then_inc(kT_psum, 1)

            def scores(g, b, i, half):
                if i == 0:
                    pe.wait_ge(kT_split, count(1, g, b, 1))
                    pe.wait_ge(q_split, count(4, g, b, (2, 4)[half]))
                width = max(256, P * (i + 1))
                cols = slice(i * P, (i + 1) * P)
                for m in HALVES[i][half]:
                    use = USE0[i] + m
                    wait_count(pe, exps_ok, count(USES, g, b, use - 2))
                    for k, h in enumerate(SHARE[i][m]):
                        s = bank[S_BANKS[use % 3]]
                        product(s[:, 256 * k:256 * k + width],
                                [(q_hi[:, b, h, cols], q_lo[:, b, h, cols], kT_hi[:, b, 0:width], kT_lo[:, b, 0:width])],
                                stop=False)
                        diagonal = 256 * k + P * i
                        last = nc.tensor.matmul(s[:, diagonal:diagonal + P], ident16[:, :], causal[:, :],
                                                start=False, stop=True)
                    last.then_inc(s_psum, 1)

            def transpose_p(g, b, i, j):
                n = TR0[i] + j
                if j == 0:
                    pe.wait_ge(prob_ok, count(4, g, b, i + 1))
                wait_count(pe, pT_split, count(TRS, g, b, n - 1))
                for h in range(G):
                    last = nc.tensor.transpose(bank[PT_BANKS[n % 2]][:, h * P:(h + 1) * P],
                                               prob[:, i % 2, h, j * P:(j + 1) * P], ident[:, :])
                last.then_inc(pT_psum, 1)

            def values(g, b, i, j):
                n = TR0[i] + j
                pe.wait_ge(pT_split, count(TRS, g, b, n + 1))
                if j == 0:
                    wait_count(pe, oT_split, count(4, g, b, i))
                a_hi, a_lo, c_hi, c_lo = v_hi[:, b, j, :], v_lo[:, b, j, :], pT_hi[:, n % 2, :], pT_lo[:, n % 2, :]
                nc.tensor.matmul(bank[OT_BANK][:, :], a_lo, c_hi, start=j == 0, stop=False)
                nc.tensor.matmul(bank[OT_BANK][:, :], a_hi, c_lo, start=False, stop=False)
                nc.tensor.matmul(bank[OT_BANK][:, :], a_hi, c_hi, start=False, stop=j == i).then_inc(pv_done, 1)

            def project_out(pg, pb, pi, h, wo_of=None):
                if h == 0:
                    if wo_of is not None:
                        pe.wait_ge(wo_split, 4 * wo_of + 4)
                    pe.wait_ge(oT_split, count(4, pg, pb, pi + 1))
                    wait_count(pe, o_added, count(4, pg, pb, pi))
                dst, k = bank[OUT_BANK][:, :], pi % 2
                nc.tensor.matmul(dst, oT_lo[:, k, h], wo_hi[:, h, :], start=h == 0, stop=False)
                nc.tensor.matmul(dst, oT_hi[:, k, h], wo_lo[:, h, :], start=False, stop=False)
                last = nc.tensor.matmul(dst, oT_hi[:, k, h], wo_hi[:, h, :], start=False, stop=h == G - 1)
                if h == G - 1:
                    last.then_inc(o_psum, 1)

            pe.wait_ge(b3_added, EXPERTS_DONE)
            project_kv(0, 0, 0, 0, True, FIRST_KV_BANKS[0])
            project_kv(0, 0, 0, 1, True, FIRST_KV_BANKS[0])
            for h in range(G):
                if h == 1:
                    project_kv(0, 0, 1, 0, True, FIRST_KV_BANKS[1])
                    project_kv(0, 0, 1, 1, True, FIRST_KV_BANKS[1])
                for c in range(HC):
                    project_q(0, 0, h, c, True, FIRST_Q_BANKS[h])
                if h == 2:
                    transpose_k(0, 0, FIRST_KT_BANK)

            def slot(g, b, i, more, begun, begun2):
                ng, nb = (g, 1) if b == 0 else (g + 1, 0)
                last, last2 = block_before(g, b, i), block_before(g, b, i, 2)
                steps_q, steps_kv, steps_out = [], [], []
                if more or b == 0:
                    steps_q = [lambda c=c: project_q(ng, nb, i, c, b == 1) for c in range(HC)]
                    if i < 2:
                        steps_kv = [lambda k=k: project_kv(ng, nb, i, k, b == 1) for k in range(2)]
                    elif i == 2:
                        steps_kv = [lambda: transpose_k(ng, nb)]
                if begun2:
                    wo_of = g if b == 0 and i == 2 else None
                    steps_out = [lambda h=h: project_out(*last2, h, wo_of) for h in range(G)]
                fill = steps_q + steps_out if i == TB - 1 else steps_kv + steps_out + steps_q
                scores(g, b, i, 0)
                n = last[2] + 1 if begun else 0
                for j in range(min(2, n)):
                    transpose_p(*last, j)
                scores(g, b, i, 1)
                for j in range(n):
                    if fill:
                        fill.pop(0)()
                    values(*last, j)
                    if j + 2 < n:
                        transpose_p(*last, j + 2)
                for work in fill:
                    work()

            def key_head(g, more, first=False):
                for n in range(B * TB):
                    slot(g, n // TB, n % TB, more, n > 0 or not first, n > 1 or not first)

            key_head(0, True, first=True)
            with pe.Fori(1, KV - 1) as g:
                key_head(g, True)
            key_head(KV - 1, False)
            last = (KV - 1, 1, TB - 1)
            transpose_p(*last, 0)
            transpose_p(*last, 1)
            for j in range(TB):
                project_out(KV - 1, 1, TB - 2, j)
                values(*last, j)
                if j + 2 < TB:
                    transpose_p(*last, j + 2)
            for h in range(G):
                project_out(*last, h)


def rotary_tables():
    half = P // 2
    inv = 1.0 / 500000.0 ** (np.arange(0, P, 2, dtype=np.float32) / P)
    wavelen = 2.0 * np.pi / inv
    scaled = np.where(wavelen > 1024.0, inv / 8.0, inv)
    smooth = (1024.0 / wavelen - 1.0) / (4.0 - 1.0)
    smoothed = (1.0 - smooth) / 8.0 * inv + smooth * inv
    medium = (wavelen <= 1024.0) & (wavelen >= 256.0)
    freq = np.where(medium, smoothed, scaled).astype(np.float32)
    angle = np.arange(T, dtype=np.float32)[:, None] * freq[None, :]
    cos, sin = np.cos(angle), np.sin(angle)
    scale = np.float32(1.0 / np.sqrt(P))
    q_cos = np.concatenate([cos.T, cos.T]) * scale
    q_sin = np.concatenate([sin.T, -sin.T]) * scale
    k_rot = np.stack([cos, -sin, sin], axis=1).reshape(TB, P, 3, half).transpose(1, 0, 2, 3)
    return [np.ascontiguousarray(a, dtype=np.float32) for a in (q_cos, q_sin, k_rot)]


def kernel(L0_attn_x, L0_attn_Wq, L0_attn_Wk, L0_attn_Wv, L0_attn_Wo, L0_ffn_router_w, L0_ffn_router_b,
           L0_ffn_router_bias, L0_ffn_ew1, L0_ffn_eb1, L0_ffn_ew2, L0_ffn_eb2, L0_ffn_ew3, L0_ffn_eb3,
           L0_ffn_sw1, L0_ffn_sb1, L0_ffn_sw2, L0_ffn_sb2, L0_ffn_sw3, L0_ffn_sb3):
    import concourse.bacc as bacc
    from concourse.bass_utils import run_bass_kernel_spmd

    def heads(w, n):
        return np.asarray(w).reshape(n, P, HC, P).transpose(0, 3, 2, 1).reshape(n, P, D)

    def halves(w):
        w = np.asarray(w)
        return np.moveaxis(w.reshape(*w.shape[:-1], 2, P), -2, 0)

    def rows(w1):
        return w1.reshape(SLOTS, HC, P, P).transpose(0, 2, 1, 3).reshape(SLOTS, P, D)

    w1 = np.concatenate([halves(L0_ffn_sw1), np.asarray(L0_ffn_ew1)])
    w2 = np.concatenate([halves(L0_ffn_sw2), np.asarray(L0_ffn_ew2)])
    w3 = np.concatenate([np.asarray(L0_ffn_sw3).reshape(2, P, D), np.asarray(L0_ffn_ew3)])
    b1 = np.concatenate([halves(L0_ffn_sb1), np.asarray(L0_ffn_eb1)])
    b2 = np.concatenate([halves(L0_ffn_sb2), np.asarray(L0_ffn_eb2)])
    q_cos, q_sin, k_rot = rotary_tables()
    arrays = {
        "x": np.asarray(L0_attn_x).reshape(B * T, D),
        "wq": heads(L0_attn_Wq, HEADS),
        "wk": heads(L0_attn_Wk, KV),
        "wv": heads(L0_attn_Wv, KV),
        "wo": np.asarray(L0_attn_Wo).T.reshape(HEADS, P, D),
        "experts": np.concatenate([rows(w1), rows(w2), w3, b1[:, :, None], b2[:, :, None]], axis=2),
        "eb3": np.concatenate([np.asarray(L0_ffn_eb3), np.asarray(L0_ffn_sb3)[None]]),
        "router_w": np.asarray(L0_ffn_router_w),
        "router_b": np.asarray(L0_ffn_router_b),
        "router_bias": np.asarray(L0_ffn_router_bias),
        "q_cos": q_cos,
        "q_sin": q_sin,
        "k_rot": k_rot,
    }
    arrays = {k: np.ascontiguousarray(a) for k, a in arrays.items()}
    nc = bacc.Bacc("TRN2", target_bir_lowering=False, num_devices=1)
    args = [nc.dram_tensor(k, a.shape, mybir.dt.from_np(a.dtype), kind="ExternalInput").ap()
            for k, a in arrays.items()]
    result = nc.dram_tensor("result", (B * T, D), F32, kind="ExternalOutput").ap()
    build(nc, *args, result)
    r = run_bass_kernel_spmd(nc, [arrays], core_ids=[0])
    return r.results[0]["result"].reshape(B, T, D)
```
